# Optimizing a Trainium2 kernel written in Bass

```python
import numpy as np
import jax
import jax.numpy as jnp

def _softmax(x, axis=-1):
    return jax.nn.softmax(x, axis=axis)

def _gelu(x):
    return jax.nn.gelu(x, approximate=True)

def _silu(x):
    return jax.nn.silu(x)

def _sigmoid(x):
    return jax.nn.sigmoid(x)

def _layernorm(x, axis=-1, eps=1e-05):
    m = jnp.mean(x, axis=axis, keepdims=True)
    v = jnp.var(x, axis=axis, keepdims=True)
    return (x - m) / jnp.sqrt(v + eps)

def _scatter_add(tgt, idx, src, axis=0):
    return tgt.at[idx].add(src)

def _segment_sum(src, seg, n):
    return jax.ops.segment_sum(src, seg, n)
kernel_name = 'mk_xattn_seq_d1_seqx_r2_34e14f'

def setup_inputs(seed: int=0):
    np.random.seed(seed)
    _w = jnp.asarray

    def _rec_inputs():
        import jax
        import jax.numpy as jnp
        _rk = jax.random.key(seed)
        x = -0.0003929 + 0.9999 * jax.random.normal(jax.random.fold_in(_rk, 1), (8, 512, 1024), jnp.float32)
        _lenS = 512 - jax.random.randint(jax.random.fold_in(_rk, 7), (8,), 0, max(1, 512 // 4) + 1, jnp.int32)
        _lenS2 = 512 - jax.random.randint(jax.random.fold_in(_rk, 8), (8,), 0, max(1, 512 // 4) + 1, jnp.int32)
        _ctx_2048P = jax.random.normal(jax.random.fold_in(_rk, 11), (8, 16, 1024), jnp.float32)
        _ctx_2048c = jax.random.dirichlet(jax.random.fold_in(_rk, 511), 0.3 * jnp.ones((16,), jnp.float32), (8, 512))
        _ctx_2048t = jnp.einsum('bsk,bkd->bsd', _ctx_2048c, _ctx_2048P)
        _ctx_2048t = _ctx_2048t * jax.lax.rsqrt(jnp.mean(jnp.square(_ctx_2048t)) + 1e-12) * 0.953939
        ctx_2048 = -8.57375e-05 + 0.999917 * (_ctx_2048t + 0.3 * jax.random.normal(jax.random.fold_in(_rk, 611), (8, 512, 1024), jnp.float32))
        _validS = jnp.arange(512)[None, :] < _lenS[:, None]
        _validS2 = jnp.arange(512)[None, :] < _lenS2[:, None]
        _causal = jnp.tril(jnp.ones((512, 512), dtype=bool))
        mask_BxS2_bf1 = jnp.ones((8, 512), dtype=bool)
        return (x, ctx_2048, mask_BxS2_bf1)
    x, ctx_2048, mask_BxS2_bf1 = _rec_inputs()

    def _L0_xattn_setup():
        import jax, jax.numpy as jnp
        import numpy as np
        HIDDEN = 1024
        HEADS = 16
        HEAD_DIM = HIDDEN // HEADS
        LN_EPS = 1e-05
        GATE_INIT = 0.5

        def _layer_norm(x, gamma, beta):
            mu = jnp.mean(x, axis=-1, keepdims=True)
            var = jnp.mean(jnp.square(x - mu), axis=-1, keepdims=True)
            return (x - mu) * jax.lax.rsqrt(var + LN_EPS) * gamma + beta
        key = jax.random.key(seed)
        ks = jax.random.split(key, 8)
        B, T_TEXT, T_AUDIO = (4, 1024, 750)
        s = 0.02
        return {'hidden_states': jax.random.normal(ks[0], (B, T_TEXT, HIDDEN), jnp.float32), 'audio_kv': jax.random.normal(ks[1], (B, T_AUDIO, HIDDEN), jnp.float32), 'audio_attention_mask': jnp.ones((B, T_AUDIO), dtype=bool), 'Wq': jax.random.normal(ks[2], (HIDDEN, HIDDEN), jnp.float32) * s, 'Wk': jax.random.normal(ks[3], (HIDDEN, HIDDEN), jnp.float32) * s, 'Wv': jax.random.normal(ks[4], (HIDDEN, HIDDEN), jnp.float32) * s, 'Wo': jax.random.normal(ks[5], (HIDDEN, HIDDEN), jnp.float32) * s, 'ln_gamma': jnp.ones((HIDDEN,), jnp.float32), 'ln_beta': jnp.zeros((HIDDEN,), jnp.float32), 'gate': jnp.array([GATE_INIT], jnp.float32)}
    _L0_xattn_all = _L0_xattn_setup()
    _L0_xattn_in = {k: v for k, v in _L0_xattn_all.items() if k in ('Wq', 'Wk', 'Wv', 'Wo', 'ln_gamma', 'ln_beta', 'gate')}
    del _L0_xattn_all
    return {'x': x, 'ctx_2048': ctx_2048, 'mask_BxS2_bf1': mask_BxS2_bf1, 'L0_xattn_Wq': _L0_xattn_in['Wq'], 'L0_xattn_Wk': _L0_xattn_in['Wk'], 'L0_xattn_Wv': _L0_xattn_in['Wv'], 'L0_xattn_Wo': _L0_xattn_in['Wo'], 'L0_xattn_ln_gamma': _L0_xattn_in['ln_gamma'], 'L0_xattn_ln_beta': _L0_xattn_in['ln_beta'], 'L0_xattn_gate': _L0_xattn_in['gate']}

def reference(x, ctx_2048, mask_BxS2_bf1, L0_xattn_Wq, L0_xattn_Wk, L0_xattn_Wv, L0_xattn_Wo, L0_xattn_ln_gamma, L0_xattn_ln_beta, L0_xattn_gate):
    import jax
    import jax.numpy as jnp

    def _L0_xattn_ref(hidden_states, audio_kv, audio_attention_mask, Wq, Wk, Wv, Wo, ln_gamma, ln_beta, gate):
        import jax, jax.numpy as jnp
        import numpy as np
        HIDDEN = 1024
        HEADS = 16
        HEAD_DIM = HIDDEN // HEADS
        LN_EPS = 1e-05
        GATE_INIT = 0.5

        def _layer_norm(x, gamma, beta):
            mu = jnp.mean(x, axis=-1, keepdims=True)
            var = jnp.mean(jnp.square(x - mu), axis=-1, keepdims=True)
            return (x - mu) * jax.lax.rsqrt(var + LN_EPS) * gamma + beta
        B, Tt, D = hidden_states.shape
        Ta = audio_kv.shape[1]
        scale = HEAD_DIM ** (-0.5)
        a = _layer_norm(audio_kv, ln_gamma, ln_beta)
        Q = (hidden_states @ Wq.T).reshape(B, Tt, HEADS, HEAD_DIM).transpose(0, 2, 1, 3)
        K = (a @ Wk.T).reshape(B, Ta, HEADS, HEAD_DIM).transpose(0, 2, 1, 3)
        V = (a @ Wv.T).reshape(B, Ta, HEADS, HEAD_DIM).transpose(0, 2, 1, 3)
        scores = jnp.einsum('bhtd,bhsd->bhts', Q, K) * scale
        mask = audio_attention_mask[:, None, None, :]
        scores = jnp.where(mask, scores, jnp.float32(-jnp.inf))
        attn = jax.nn.softmax(scores, axis=-1)
        out = jnp.einsum('bhts,bhsd->bhtd', attn, V)
        out = out.transpose(0, 2, 1, 3).reshape(B, Tt, D)
        out = out @ Wo.T
        return hidden_states + jnp.tanh(gate) * out
    x = _L0_xattn_ref(x, ctx_2048, mask_BxS2_bf1, L0_xattn_Wq, L0_xattn_Wk, L0_xattn_Wv, L0_xattn_Wo, L0_xattn_ln_gamma, L0_xattn_ln_beta, L0_xattn_gate)
    return x

_drawn_inputs = setup_inputs


def setup_inputs(seed=0):
    import zlib

    import numpy as np

    out = dict(_drawn_inputs(seed))
    spreads = {'L0_xattn_ln_gamma': (1.0, 0.6), 'L0_xattn_ln_beta': (0.0, 0.428)}
    factors = {'L0_xattn_Wq': 4.139, 'L0_xattn_Wk': 4.16}
    for name, (base, spread) in spreads.items():
        noise = np.random.default_rng([zlib.crc32(name.encode()), seed]).standard_normal(out[name].shape)
        drawn = base * np.exp(spread * noise) if base else spread * noise
        out[name] = jnp.asarray(drawn.astype(out[name].dtype))
    for name, factor in factors.items():
        out[name] = (out[name] * factor).astype(out[name].dtype)
    return out
```

```python
from contextlib import ExitStack

import numpy as np

import concourse.bass as bass
from concourse import mybir

F32 = mybir.dt.float32
F32R = mybir.dt.float32r
U8 = mybir.dt.uint8
ACT = mybir.ActivationFunctionType
ALU = mybir.AluOpType

P = 128
B, T, D = 8, 512, 1024
HD = 64
KT = D // P
PAIRS = D // P
TB = T // P
UNITS = 2 * TB
CH = 4
SCALE = HD ** -0.5
EPS = 1e-5
BIG = 3.0e38
WQ, WK, WV, WO = range(4)
LAST = B * PAIRS - 1


def xattn_kernel(nc, xT, ctx, mask, wts, gamma, beta, gate, yT):
    es = ExitStack()
    with es:
        def sb(name, shape, dt=F32):
            return es.enter_context(nc.sbuf_tensor(name, shape, dt))

        def bank(name):
            return es.enter_context(nc.psum_tensor(name, [P, T], F32))

        def sem(name):
            return es.enter_context(nc.semaphore(name))

        xy = sb("xy", [P, 2, KT, T])
        cx = sb("cx", [P, TB, D])
        x_hi, x_lo = sb("x_hi", [P, KT, T], F32R), sb("x_lo", [P, KT, T], F32R)
        a_hi, a_lo = sb("a_hi", [P, KT, T], F32R), sb("a_lo", [P, KT, T], F32R)
        w_raw = sb("w_raw", [P, 2, D])
        w_hi, w_lo = sb("w_hi", [P, 4, D], F32R), sb("w_lo", [P, 4, D], F32R)
        q_st = sb("q_st", [P, 2, T], F32R)
        k_st = sb("k_st", [P, 2, 2, T], F32R)
        vt = sb("vt", [P, T])
        v_st = sb("v_st", [P, TB, 4, HD], F32R)
        prob = sb("prob", [P, UNITS, T])
        pt_hi, pt_lo = sb("pt_hi", [P, 2, T], F32R), sb("pt_lo", [P, 2, T], F32R)
        o_tmp, o32 = sb("o_tmp", [P, T]), sb("o32", [P, T])
        o_hi, o_lo = sb("o_hi", [P, T], F32R), sb("o_lo", [P, T], F32R)
        mask_u8 = sb("mask_u8", [P, T], U8)
        mask_add = sb("mask_add", [P, T])
        ident = sb("ident", [P, P])
        nmax, rsum, rinv = sb("nmax", [P, UNITS]), sb("rsum", [P, UNITS]), sb("rinv", [P, UNITS])
        bn = sb("bn", [P, TB, 2, 6])
        mv = sb("mv", [P, TB, 2])
        nmean, vpe, rstd, nhalf = (sb(n, [P, TB]) for n in ("nmean", "vpe", "rstd", "nhalf"))
        gam, bet = sb("gam", [P, KT]), sb("bet", [P, KT])
        gate_in, tg = sb("gate_in", [P, 1]), sb("tg", [P, 1])

        so = [bank("so0"), bank("so1")]
        pt = [bank("pt0"), bank("pt1")]
        pv = [bank("pv0"), bank("pv1")]
        pj = [bank("pj0"), bank("pj1")]

        const_ld, x_ld, ctx_ld, mask_ld = sem("const_ld"), sem("x_ld"), sem("ctx_ld"), sem("mask_ld")
        w_ld = [sem("w_ld0"), sem("w_ld1")]
        y_st = sem("y_st")
        so_read = sem("so_read")
        pl_done = sem("pl_done")
        rinv_done, ql_done, kl_done, vl_done = sem("rinv_done"), sem("ql_done"), sem("kl_done"), sem("vl_done")
        oadd_done, ol_done = sem("oadd_done"), sem("ol_done")
        mask_done, bn_done, stat_done = sem("mask_done"), sem("bn_done"), sem("stat_done")
        xlv_done, alv_done = sem("xlv_done"), sem("alv_done")
        tg_done, exp_done, vt_done, vh_done = sem("tg_done"), sem("exp_done"), sem("vt_done"), sem("vh_done")
        qh_done, kh_done, ph_done = sem("qh_done"), sem("kh_done"), sem("ph_done")
        otmp_done, oh_done, whi_done = sem("otmp_done"), sem("oh_done"), sem("whi_done")
        xh_done, at_done, ah_done = sem("xh_done"), sem("at_done"), sem("ah_done")
        ident_done, nhalf_done, scale_done, wlo_done = (
            sem("ident_done"), sem("nhalf_done"), sem("scale_done"), sem("wlo_done"))
        rstd_done, z_done, xlp_done, alp_done = sem("rstd_done"), sem("z_done"), sem("xlp_done"), sem("alp_done")
        s_done, vtr_done, t_done, pv_done, op_done = (
            sem("s_done"), sem("vtr_done"), sem("t_done"), sem("pv_done"), sem("op_done"))
        q_done, k_done, v_done, ct_done = sem("q_done"), sem("k_done"), sem("v_done"), sem("ct_done")

        def f32(ap):
            return ap.bitcast(F32)

        def at(i, n=1):
            v = cx[:, :, i * P:(i + n) * P].rearrange("p s (k t) -> p k s t", k=n)
            return v[:, 0] if n == 1 else v

        def blocks(ap):
            return ap.rearrange("p k (s t) -> p k s t", s=TB)

        lo_half, hi_half = slice(0, HD), slice(HD, P)

        def w_number(kind, k):
            return 4 * k + {WV: 5, WO: 6, WQ: 7, WK: 8}[kind]

        def w_slot(kind):
            return 1 if kind in (WV, WQ) else 0

        def w_loaded(kind, k):
            return 16 * (2 * k + {WV: 3, WQ: 4, WO: 4, WK: 5}[kind])

        block = es.enter_context(nc.Block())

        def run_loops(eng, body, top=None, bottom=None):
            with eng.Fori(0, B - 1) as b:
                if top:
                    top(b)
                with eng.Fori(0, PAIRS - 2) as j:
                    body(b * PAIRS + j, b, j, "plain")
                body(b * PAIRS + (PAIRS - 2), b, PAIRS - 2, "prepare")
                body(b * PAIRS + (PAIRS - 1), b, PAIRS - 1, "switch")
                if bottom:
                    bottom(b)
            with eng.Fori(0, PAIRS - 2) as j:
                body(j + (B - 1) * PAIRS, B - 1, j, "plain")
            body(LAST - 1, B - 1, PAIRS - 2, "plain")
            body(LAST, B - 1, PAIRS - 1, "last")
            if bottom:
                bottom(B - 1)

        @block.sync
        def _(sp):
            def load_w(kind, j, k):
                m, s = w_number(kind, k), w_slot(kind)
                sp.wait_ge(wlo_done, m - 1)
                sp.nop(nofuse=True)
                sp.dma_start(w_raw[:, s], wts[kind][bass.ds(j, 1)].rearrange("a p n -> p (a n)")).then_inc(w_ld[s], 16)

            def load_x(b, parity):
                sp.dma_start(xy[:, bass.ds(parity, 1)].rearrange("p a k t -> p (a k t)"),
                             xT[bass.ds(b, 1)].rearrange("a p n -> p (a n)")).then_inc(x_ld, 16)

            def load_ctx(b):
                sp.dma_start(cx[:], ctx[bass.ds(b, 1)].rearrange("a (s p) d -> p (a s) d", p=P)).then_inc(ctx_ld, 16)

            def load_mask(b):
                sp.dma_start(mask_u8[:], mask[bass.ds(b, 1), :].to_broadcast((P, T))).then_inc(mask_ld, 16)

            sp.sem_inc(y_st, 16)
            load_ctx(0)
            sp.dma_start(w_raw[:, 0], wts[WQ][0]).then_inc(w_ld[0], 16)
            load_x(0, 0)
            sp.dma_start(w_raw[:, 1], wts[WK][0]).then_inc(w_ld[1], 16)
            load_mask(0)
            sp.dma_start(gam[:], gamma).then_inc(const_ld, 16)
            sp.dma_start(bet[:], beta).then_inc(const_ld, 16)
            sp.dma_start(gate_in[:], gate.to_broadcast((P, 1))).then_inc(const_ld, 16)
            for m, (kind, j) in enumerate([(WV, 0), (WQ, 1), (WK, 1)], 2):
                sp.wait_ge(wlo_done, m - 1)
                sp.dma_start(w_raw[:, m % 2], wts[kind][j]).then_inc(w_ld[m % 2], 16)

            def top(b):
                sp.wait_ge(y_st, b * 16 + 16)
                sp.nop(nofuse=True)
                load_x(b + 1, (b + 1) % 2)
                sp.wait_ge(alv_done, b * 2 + 2)
                sp.wait_ge(alp_done, b * 2 + 2)
                sp.nop(nofuse=True)
                load_ctx(b + 1)
                sp.wait_ge(mask_done, b * 2 + 2)
                sp.nop(nofuse=True)
                load_mask(b + 1)

            def body(k, b, j, kind):
                if kind == "last":
                    return load_w(WO, j, k)
                load_w(WV, (j + 1) % PAIRS if isinstance(j, int) else j + 1, k)
                load_w(WO, j, k)
                load_w(WQ, (j + 2) % PAIRS if isinstance(j, int) else j + 2, k)
                load_w(WK, (j + 2) % PAIRS if isinstance(j, int) else j + 2, k)

            def bottom(b):
                sp.wait_ge(so_read, (b + 1) * (16 * PAIRS) + 2)
                sp.nop(nofuse=True)
                sp.dma_start(yT[bass.ds(b, 1)].rearrange("a p n -> p (a n)"),
                             xy[:, bass.ds(b % 2, 1)].rearrange("p a k t -> p (a k t)")).then_inc(y_st, 16)

            run_loops(sp, body, top, bottom)
            sp.wait_ge(y_st, 16 * B + 16)

        @block.tensor
        def _(pe):
            def scores(k, u):
                h, t = divmod(u, TB)
                if u == 0:
                    pe.wait_ge(ql_done, k * 2 + 2)
                    pe.wait_ge(kl_done, k * 4 + 4)
                    pe.wait_ge(kh_done, k * 4 + 4)
                pe.wait_ge(so_read, k * 16 + (u + 1))
                for order in range(2):
                    mm = pe.matmul(so[u % 2][:], q_st[:, h, t * P:(t + 1) * P], k_st[:, h, order],
                                   start=order == 0, stop=order == 1)
                mm.then_inc(s_done, 1)

            def turn_v(k):
                pe.wait_ge(vt_done, k + 1)
                pe.wait_ge(ident_done, 2)
                for s in range(TB):
                    mm = pe.transpose(pj[0][:, s * P:(s + 1) * P], vt[:, s * P:(s + 1) * P], ident[:])
                mm.then_inc(vtr_done, 1)

            def turn_p(k, u, kind):
                h, s = divmod(u, TB)
                if s == 0:
                    pe.wait_ge(scale_done, k * UNITS + TB * (h + 1))
                pe.wait_ge(pl_done, k * UNITS + (u + 1))
                for t in range(TB):
                    mm = pe.transpose(pt[u % 2][:, t * P:(t + 1) * P], prob[:, h * TB + t, s * P:(s + 1) * P],
                                      ident[:])
                mm.then_inc(t_done, 1)

            def values(k, u):
                h, s = divmod(u, TB)
                if s == 0:
                    pe.wait_ge(vl_done, k + 1)
                pe.wait_ge(pl_done, k * UNITS + (u + 3))
                w = v_st[:, s, 2 * h:2 * h + 2].rearrange("p a d -> p (a d)")
                pe.matmul(pv[h][:], w, pt_hi[:, u % 2], start=s == 0, stop=False)
                pe.matmul(pv[h][:], w, pt_lo[:, u % 2], start=False, stop=s == TB - 1).then_inc(pv_done, 1)

            def partial_out(k, n, kind):
                if n == 0:
                    pe.wait_ge(ol_done, k + 1)
                    pe.wait_ge(wlo_done, w_number(WO, k) + (0 if kind == "last" else 1))
                pe.wait_ge(so_read, k * 16 + (UNITS + n + 1))
                cols = slice(n * P, (n + 1) * P)
                pe.matmul(so[n % 2][:], w_hi[:, WO, cols], o_hi[:], start=True, stop=False)
                pe.matmul(so[n % 2][:], w_hi[:, WO, cols], o_lo[:], start=False, stop=False)
                pe.matmul(so[n % 2][:], w_lo[:, WO, cols], o_hi[:], start=False, stop=True).then_inc(op_done, 1)

            def projections(k, b, kind):
                first = isinstance(k, int) and k == -1
                for w, dst, done, s_hi, s_lo in ((WQ, pj[1], q_done, x_hi, x_lo), (WK, pj[0], k_done, a_hi, a_lo),
                                                 (WV, pj[1], v_done, a_hi, a_lo)):
                    if first:
                        pe.wait_ge(wlo_done, w + 1)
                        if w == WV:
                            pe.wait_ge(ql_done, 2)
                    elif w == WQ:
                        pe.wait_ge(wlo_done, k * 4 + 4)
                        pe.wait_ge(vt_done, k + 1)
                    elif w == WK:
                        pe.wait_ge(wlo_done, k * 4 + 5)
                        pe.wait_ge(vl_done, k + 1)
                    else:
                        pe.wait_ge(wlo_done, k * 4 + 6)
                        pe.wait_ge(ql_done, k * 2 + 4)
                    for i in range(KT):
                        if kind == "switch" and i % 2 == 0 and w != WV:
                            c = i // 2
                            by_v, by_p = (xlv_done, xlp_done) if w == WQ else (alv_done, alp_done)
                            if c < 2:
                                pe.wait_ge(by_v, b * 2 + (2 + c + 1))
                            else:
                                pe.wait_ge(by_p, b * 2 + (2 + c - 1))
                        cols = slice(i * P, (i + 1) * P)
                        pe.matmul(dst[:], w_hi[:, w, cols], s_hi[:, i], start=i == 0, stop=False)
                        yield
                        pe.matmul(dst[:], w_hi[:, w, cols], s_lo[:, i], start=False, stop=False)
                        yield
                        mm = pe.matmul(dst[:], w_lo[:, w, cols], s_hi[:, i], start=False, stop=i == KT - 1)
                        if i == KT - 1:
                            mm.then_inc(done, 1)
                        yield

            def turn_ctx(k, b, i):
                if i == 0:
                    pe.wait_ge(z_done, b * TB + 2 * TB)
                if i < 2 and not (isinstance(k, int) and k == -1):
                    pe.wait_ge(pl_done, k * UNITS + (UNITS + 2))
                if i >= 2:
                    pe.wait_ge(at_done, b * KT + (KT + i - 1))
                for s in range(TB):
                    mm = pe.transpose(pt[i % 2][:, s * P:(s + 1) * P], cx[:, s, i * P:(i + 1) * P], ident[:])
                mm.then_inc(ct_done, 1)

            def take(stream, n):
                for _ in range(n):
                    next(stream, None)

            def body(k, b, j, kind):
                stream = iter(()) if kind == "last" else projections(k, b, kind)
                for u in range(UNITS):
                    scores(k, u)
                    if u == 1:
                        turn_v(k)
                    take(stream, (0, 3, 3, 3, 3, 3, 3, 6)[u])
                if kind == "switch":
                    pe.wait_ge(at_done, b * KT + 2 * KT)
                for u in range(UNITS):
                    turn_p(k, u, kind)
                    take(stream, 2)
                    if u:
                        values(k, u - 1)
                take(stream, 4)
                values(k, UNITS - 1)
                take(stream, 12)
                for n in range(KT):
                    partial_out(k, n, kind)
                    take(stream, 2)
                    if kind == "prepare":
                        turn_ctx(k, b, n)

            stream = projections(-1, -1, "switch")
            take(stream, 3 * KT)
            pe.wait_ge(ident_done, 2)
            for i in range(KT):
                turn_ctx(-1, -1, i)
            take(stream, 6 * KT)
            run_loops(pe, body)

        @block.scalar
        def _(act):
            def split_w(kind, k, number=None):
                s = w_slot(kind)
                act.wait_ge(w_ld[s], w_loaded(kind, k))
                if kind == WQ:
                    act.wait_ge(q_done, k + 2)
                if kind == WK:
                    act.wait_ge(k_done, k + 2)
                act.copy(w_hi[:, kind], w_raw[:, s]).then_inc(whi_done, 1)

            def copy_vt(k):
                act.wait_ge(v_done, k + 1)
                act.copy(vt[:], pj[1][:]).then_inc(vt_done, 1)

            def exp(k, u):
                act.wait_ge(so_read, k * 16 + (u + 3))
                act.activation(prob[:, u], prob[:, u], ACT.Exp, bias=nmax[:, u:u + 1], scale=-1.0,
                               accum_out=rsum[:, u:u + 1]).then_inc(exp_done, 1)

            def v_high(k):
                act.wait_ge(vtr_done, k + 1)
                act.copy(v_st[:, :, 0:4:3], pj[0][:].rearrange("p (s h d) -> p s h d", s=TB, h=2)).then_inc(vh_done, 1)

            def q_high(k, h):
                if h == 0:
                    act.wait_ge(q_done, k + 2)
                half = hi_half if h else lo_half
                act.copy(q_st[half, h], pj[1][half]).then_inc(qh_done, 1)

            def k_high(k, i):
                h, order = i % 2, i // 2
                if i == 0:
                    act.wait_ge(k_done, k + 2)
                src = hi_half if h else lo_half
                dst = src if order == 0 else (lo_half if h else hi_half)
                act.copy(k_st[dst, h, order], pj[0][src]).then_inc(kh_done, 1)

            def p_high(k, u):
                act.wait_ge(t_done, k * UNITS + (u + 1))
                act.copy(pt_hi[:, u % 2], pt[u % 2][:]).then_inc(ph_done, 1)

            def o_move(k, h):
                act.wait_ge(pv_done, k * UNITS + TB * (h + 1))
                src, dst = (lo_half, hi_half) if h else (hi_half, lo_half)
                act.copy(o_tmp[dst], pv[h][src]).then_inc(otmp_done, 1)

            def o_high(k):
                act.wait_ge(oadd_done, k * 2 + 2)
                act.copy(o_hi[:], o32[:]).then_inc(oh_done, 1)

            def x_high(k, b, c, parity):
                if c == 0:
                    act.wait_ge(x_ld, b * 16 + 32)
                    if not isinstance(k, int):
                        act.wait_ge(q_done, k + 2)
                    act.nop(nofuse=True)
                act.copy(x_hi[:, 2 * c:2 * c + 2].rearrange("p k t -> p (k t)"),
                         xy[:, bass.ds(parity, 1), 2 * c:2 * c + 2].rearrange("p a k t -> p (a k t)")
                         ).then_inc(xh_done, 1)

            def a_float(b, i):
                act.wait_ge(ct_done, b * KT + (KT + i + 1))
                act.activation(at(i), pt[i % 2][:].rearrange("p (s t) -> p s t", s=TB), ACT.Identity,
                               bias=bet[:, i:i + 1], scale=gam[:, i:i + 1]).then_inc(at_done, 1)

            def a_high(b, c):
                if c == 0:
                    act.wait_ge(at_done, b * KT + 2 * KT)
                act.copy(blocks(a_hi[:, 2 * c:2 * c + 2]), at(2 * c, 2)).then_inc(ah_done, 1)

            def body(k, b, j, kind):
                last = kind == "last"
                copy_vt(k)
                exp(k, 0)
                exp(k, 1)
                v_high(k)
                for u in range(2, UNITS):
                    exp(k, u)
                    if kind == "switch" and u >= 4:
                        a_high(b, u - 4)
                    if u == 3 and not last:
                        split_w(WV, k)
                for u in range(UNITS):
                    p_high(k, u)
                    if u in (1, 2) and not last:
                        q_high(k, u - 1)
                    if u == 3:
                        split_w(WO, k)
                    if u == 5:
                        o_move(k, 0)
                    if kind == "prepare" and u >= 4:
                        x_high(k, b, u - 4, (b + 1) % 2)
                o_move(k, 1)
                o_high(k)
                if last:
                    return
                for i in range(4):
                    k_high(k, i)
                if kind == "prepare":
                    for i in range(2):
                        a_float(b, i)
                split_w(WQ, k)
                if kind == "prepare":
                    for i in range(2, KT):
                        a_float(b, i)
                split_w(WK, k)

            act.wait_ge(w_ld[0], 16)
            act.copy(w_hi[:, WQ], w_raw[:, 0]).then_inc(whi_done, 1)
            for c in range(CH):
                x_high(-1, -1, c, 0)
            act.wait_ge(w_ld[1], 16)
            act.copy(w_hi[:, WK], w_raw[:, 1]).then_inc(whi_done, 1)
            act.wait_ge(const_ld, 48)
            act.activation(tg[:], gate_in[:], ACT.Tanh).then_inc(tg_done, 1)
            for i in range(KT):
                a_float(-1, i)
            for c in range(CH):
                a_high(-1, c)
            act.wait_ge(w_ld[0], 32)
            act.copy(w_hi[:, WV], w_raw[:, 0]).then_inc(whi_done, 1)
            q_high(-1, 0)
            q_high(-1, 1)
            act.wait_ge(w_ld[1], 32)
            act.copy(w_hi[:, WQ], w_raw[:, 1]).then_inc(whi_done, 1)
            for i in range(4):
                k_high(-1, i)
            act.wait_ge(w_ld[0], 48)
            act.copy(w_hi[:, WK], w_raw[:, 0]).then_inc(whi_done, 1)
            run_loops(act, body)

        @block.vector
        def _(dve):
            def row_max(k, u):
                dve.wait_ge(s_done, k * UNITS + (u + 1))
                dve.nop(nofuse=True)
                dve.wait_ge(mask_done, 2)
                dve.tensor_tensor_reduce(prob[:, u], so[u % 2][:], mask_add[:], -SCALE, BIG, ALU.add, ALU.min,
                                         nmax[:, u:u + 1]).then_inc(so_read, 1)

            def inverse_sums(k, i):
                dve.wait_ge(exp_done, k * UNITS + 2 * (i + 1))
                dve.reciprocal(rinv[:, 2 * i:2 * i + 2], rsum[:, 2 * i:2 * i + 2]).then_inc(rinv_done, 1)

            def v_low(k):
                dve.wait_ge(vh_done, k + 1)
                dve.tensor_tensor(v_st[:, :, 1:3], pj[0][:].rearrange("p (s h d) -> p s h d", s=TB, h=2),
                                  f32(v_st[:, :, 0:4:3]), ALU.subtract).then_inc(vl_done, 1)

            def q_low(k, h):
                if h == 0:
                    dve.wait_ge(qh_done, k * 2 + 4)
                src, dst = (hi_half, lo_half) if h else (lo_half, hi_half)
                dve.tensor_tensor(q_st[dst, h], pj[1][src], f32(q_st[src, h]), ALU.subtract).then_inc(ql_done, 1)

            def k_low(k, i):
                h, order = i % 2, 1 - i // 2
                if i == 0:
                    dve.wait_ge(kh_done, k * 4 + 8)
                src = hi_half if h else lo_half
                dst = src if order == 1 else (lo_half if h else hi_half)
                dve.tensor_tensor(k_st[dst, h, order], pj[0][src], f32(k_st[src, h, 0]),
                                  ALU.subtract).then_inc(kl_done, 1)

            def p_low(k, u):
                dve.wait_ge(ph_done, k * UNITS + (u + 1))
                dve.tensor_tensor(pt_lo[:, u % 2], pt[u % 2][:], f32(pt_hi[:, u % 2]),
                                  ALU.subtract).then_inc(pl_done, 1)

            def o_add(k, h):
                dve.wait_ge(otmp_done, k * 2 + (h + 1))
                rows = hi_half if h else lo_half
                dve.tensor_tensor(o32[rows], pv[h][rows], o_tmp[rows], ALU.add).then_inc(oadd_done, 1)

            def o_low(k):
                dve.wait_ge(oh_done, k + 1)
                dve.tensor_tensor(o_lo[:], o32[:], f32(o_hi[:]), ALU.subtract).then_inc(ol_done, 1)

            def accumulate(k, n, parity):
                dve.wait_ge(op_done, k * KT + (n + 1))
                y = xy[:, bass.ds(parity, 1), n].rearrange("p a t -> p (a t)")
                dve.scalar_tensor_tensor(out=y, in0=so[n % 2][:], scalar=tg[:], in1=y,
                                         op0=ALU.mult, op1=ALU.add).then_inc(so_read, 1)

            def x_low(b, c, parity):
                dve.wait_ge(xh_done, b * CH + (CH + c + 1))
                dve.tensor_tensor(x_lo[:, 2 * c:2 * c + 2].rearrange("p k t -> p (k t)"),
                                  xy[:, bass.ds(parity, 1), 2 * c:2 * c + 2].rearrange("p a k t -> p (a k t)"),
                                  f32(x_hi[:, 2 * c:2 * c + 2]).rearrange("p k t -> p (k t)"),
                                  ALU.subtract).then_inc(xlv_done, 1)

            def a_low(b, c):
                dve.wait_ge(ah_done, b * CH + (CH + c + 1))
                dve.tensor_tensor(blocks(a_lo[:, 2 * c:2 * c + 2]), at(2 * c, 2), f32(blocks(a_hi[:, 2 * c:2 * c + 2])),
                                  ALU.subtract).then_inc(alv_done, 1)

            def build_mask(b):
                dve.wait_ge(mask_ld, b * 16 + 32)
                dve.tensor_scalar(mask_add[:], mask_u8[:], -1.0, BIG, ALU.add, ALU.mult).then_inc(mask_done, 1)
                dve.wait_ge(mask_done, b * 2 + 3)
                dve.tensor_scalar(mask_add[:], mask_add[:], BIG, None, ALU.mult).then_inc(mask_done, 1)
                dve.wait_ge(mask_done, b * 2 + 4)

            def row_stats(b):
                dve.wait_ge(ctx_ld, b * 16 + 32)
                for s in range(TB):
                    for half in range(2):
                        dve.bn_stats(bn[:, s, half], cx[:, s, half * T:(half + 1) * T]).then_inc(bn_done, 1)

            def row_moments(b):
                dve.wait_ge(bn_done, b * 3 * TB + 5 * TB)
                dve.nop(nofuse=True)
                for s in range(TB):
                    dve.bn_aggr(mv[:, s], bn[:, s].rearrange("p a c -> p (a c)")).then_inc(bn_done, 1)
                dve.wait_ge(bn_done, b * 3 * TB + 6 * TB)
                dve.tensor_scalar(nmean[:], mv[:, :, 0], -1.0, None, ALU.mult).then_inc(stat_done, 1)
                dve.tensor_scalar(vpe[:], mv[:, :, 1], EPS, None, ALU.add).then_inc(stat_done, 1)

            def body(k, b, j, kind):
                last = kind == "last"
                parity = b % 2
                for u in range(UNITS):
                    row_max(k, u)
                    if u == 1:
                        v_low(k)
                    if u in (3, 5, 7):
                        inverse_sums(k, (u - 3) // 2)
                inverse_sums(k, 3)
                if kind == "prepare":
                    row_stats(b)
                    row_moments(b)
                if kind == "switch":
                    a_low(b, 0)
                    a_low(b, 1)
                for u in range(UNITS):
                    p_low(k, u)
                    if u in (2, 3) and not last:
                        q_low(k, u - 2)
                    if u == 5:
                        o_add(k, 0)
                    if kind == "switch" and u == 4:
                        build_mask(b)
                o_add(k, 1)
                o_low(k)
                for n in range(KT):
                    accumulate(k, n, parity)
                    if kind == "prepare" and n in (0, 1):
                        x_low(b, n, (b + 1) % 2)
                    if 1 <= n <= 4 and not last:
                        k_low(k, n - 1)

            for i, s in enumerate((pl_done, pl_done, so_read, so_read)):
                dve.memset(nmax[:, i:i + 1], 0.0).then_inc(s, 1)
            build_mask(-1)
            row_stats(-1)
            row_moments(-1)
            x_low(-1, 0, 0)
            x_low(-1, 1, 0)
            dve.wait_ge(tg_done, 1)
            a_low(-1, 0)
            a_low(-1, 1)
            q_low(-1, 0)
            q_low(-1, 1)
            for i in range(4):
                k_low(-1, i)
            run_loops(dve, body)

        @block.gpsimd
        def _(pool):
            def scale_rows(k, u):
                if u % 2 == 0:
                    pool.wait_ge(rinv_done, k * 4 + (u // 2 + 1))
                    pool.nop(nofuse=True)
                pool.tensor_scalar(prob[:, u], prob[:, u], rinv[:, u:u + 1], 1.0, ALU.mult,
                                   ALU.mult).then_inc(scale_done, 1)

            def split_w(kind, k, less=0):
                pool.wait_ge(whi_done, w_number(kind, k) + (1 - less))
                pool.tensor_tensor(w_lo[:, kind], w_raw[:, w_slot(kind)], f32(w_hi[:, kind]),
                                   ALU.subtract).then_inc(wlo_done, 1)

            def norm_rows(b):
                pool.wait_ge(stat_done, b * 2 + 4)
                pool.tensor_tensor(rstd[:], vpe[:], nhalf[:], ALU.pow).then_inc(rstd_done, 1)
                pool.wait_ge(rstd_done, b + 2)
                pool.nop(nofuse=True)
                for s in range(TB):
                    pool.tensor_scalar(cx[:, s], cx[:, s], nmean[:, s:s + 1], rstd[:, s:s + 1], ALU.add,
                                       ALU.mult).then_inc(z_done, 1)

            def x_low(b, c, parity):
                pool.wait_ge(xh_done, b * CH + (CH + c + 1))
                pool.nop(nofuse=True)
                pool.tensor_tensor(x_lo[:, 2 * c:2 * c + 2].rearrange("p k t -> p (k t)"),
                                   xy[:, bass.ds(parity, 1), 2 * c:2 * c + 2].rearrange("p a k t -> p (a k t)"),
                                   f32(x_hi[:, 2 * c:2 * c + 2]).rearrange("p k t -> p (k t)"),
                                   ALU.subtract).then_inc(xlp_done, 1)

            def a_low(b, c):
                pool.wait_ge(ah_done, b * CH + (CH + c + 1))
                pool.tensor_tensor(blocks(a_lo[:, 2 * c:2 * c + 2]), at(2 * c, 2),
                                   f32(blocks(a_hi[:, 2 * c:2 * c + 2])), ALU.subtract).then_inc(alp_done, 1)

            def body(k, b, j, kind):
                for u in range(UNITS):
                    scale_rows(k, u)
                if kind == "last":
                    return split_w(WO, k, less=1)
                if kind == "prepare":
                    norm_rows(b)
                if kind == "switch":
                    a_low(b, 2)
                    a_low(b, 3)
                split_w(WV, k)
                split_w(WO, k)
                if kind == "prepare":
                    x_low(b, 2, (b + 1) % 2)
                    x_low(b, 3, (b + 1) % 2)
                split_w(WQ, k)
                split_w(WK, k)

            pool.memset(ident[:], 0.0).then_inc(ident_done, 1)
            pool.memset(nhalf[:], -0.5).then_inc(nhalf_done, 1)
            pool.wait_ge(ident_done, 1)
            pool.affine_select(out=ident[:], in_=ident[:], compare_op=ALU.not_equal, fill=1.0, base=0,
                               pattern=[[-1, P]], channel_multiplier=1).then_inc(ident_done, 1)
            pool.wait_ge(nhalf_done, 1)

            def split_first(m, kind):
                pool.wait_ge(whi_done, m + 1)
                pool.tensor_tensor(w_lo[:, kind], w_raw[:, m % 2], f32(w_hi[:, kind]),
                                   ALU.subtract).then_inc(wlo_done, 1)

            split_first(0, WQ)
            x_low(-1, 2, 0)
            x_low(-1, 3, 0)
            norm_rows(-1)
            split_first(1, WK)
            a_low(-1, 2)
            a_low(-1, 3)
            for m, kind in ((2, WV), (3, WQ), (4, WK)):
                split_first(m, kind)
            run_loops(pool, body)


def kernel(**inputs):
    import concourse.bacc as bacc
    from concourse.bass_utils import run_bass_kernel_spmd

    def arr(name):
        return np.asarray(inputs[name])

    def lay(a):
        return np.ascontiguousarray(a)

    def projection(w):
        return lay(w.reshape(PAIRS, P, KT, P).transpose(0, 3, 2, 1)).reshape(PAIRS, P, D)

    arrays = {
        "xT": lay(arr("x").reshape(B, T, KT, P).transpose(0, 3, 2, 1)).reshape(B, P, KT * T),
        "ctx": lay(arr("ctx_2048")),
        "mask": lay(arr("mask_BxS2_bf1")).view(np.uint8),
        "wq": projection(arr("L0_xattn_Wq")),
        "wk": projection(arr("L0_xattn_Wk")),
        "wv": projection(arr("L0_xattn_Wv")),
        "wo": lay(arr("L0_xattn_Wo").T).reshape(PAIRS, P, D),
        "gamma": lay(arr("L0_xattn_ln_gamma").reshape(KT, P).T),
        "beta": lay(arr("L0_xattn_ln_beta").reshape(KT, P).T),
        "gate": lay(arr("L0_xattn_gate").reshape(1, 1)),
    }
    nc = bacc.Bacc("TRN2", target_bir_lowering=False, num_devices=1)
    t = {n: nc.dram_tensor(f"in_{n}", a.shape, mybir.dt.from_np(a.dtype), kind="ExternalInput").ap()
         for n, a in arrays.items()}
    y = nc.dram_tensor("out_y", (B, P, KT * T), F32, kind="ExternalOutput").ap()
    xattn_kernel(nc, t["xT"], t["ctx"], t["mask"], [t["wq"], t["wk"], t["wv"], t["wo"]],
                 t["gamma"], t["beta"], t["gate"], y)
    r = run_bass_kernel_spmd(nc, [{f"in_{n}": a for n, a in arrays.items()}], core_ids=[0])
    out = np.asarray(r.results[0]["out_y"]).reshape(B, P, KT, T).transpose(0, 3, 2, 1)
    return np.ascontiguousarray(out).reshape(B, T, D)
```

```python
from contextlib import ExitStack

import numpy as np

import concourse.bass as bass
from concourse import mybir

F32 = mybir.dt.float32
F32R = mybir.dt.float32r
U8 = mybir.dt.uint8
ACT = mybir.ActivationFunctionType
ALU = mybir.AluOpType

P = 128
B, T, D = 8, 512, 1024
HD = 64
KT = D // P
PAIRS = D // P
TB = T // P
UNITS = 2 * TB
BY_V = KT // 2
SCALE = HD ** -0.5
EPS = 1e-5
BIG = 3.0e38
WQ, WK, WV, WO = range(4)
LAST = B * PAIRS - 1
FILL_S = (0, 4, 4, 4, 4, 4, 5, 5)
FILL_T = (4, 2, 2, 2, 2, 2, 2, 2)
FILL_GAP = (4, 12)
FILL_O = (1, 1, 1, 1, 1, 1, 2, 0)
assert sum(FILL_S) + sum(FILL_T) + sum(FILL_GAP) + sum(FILL_O) == 3 * 3 * KT


def xattn_kernel(nc, xT, ctx, mask, wts, gamma, beta, gate, yT):
    es = ExitStack()
    with es:
        def sb(name, shape, dt=F32):
            return es.enter_context(nc.sbuf_tensor(name, shape, dt))

        def bank(name):
            return es.enter_context(nc.psum_tensor(name, [P, T], F32))

        def sem(name):
            return es.enter_context(nc.semaphore(name))

        xy = sb("xy", [P, 2, KT, T])
        cx = sb("cx", [P, TB, D])
        x_hi, x_lo = sb("x_hi", [P, KT, T], F32R), sb("x_lo", [P, KT, T], F32R)
        a_hi, a_lo = sb("a_hi", [P, KT, T], F32R), sb("a_lo", [P, KT, T], F32R)
        w_raw = sb("w_raw", [P, 2, D])
        w_hi, w_lo = sb("w_hi", [P, 4, D], F32R), sb("w_lo", [P, 4, D], F32R)
        q_st = sb("q_st", [P, 2, T], F32R)
        k_st = sb("k_st", [P, 2, 2, T], F32R)
        vt = sb("vt", [P, T])
        v_st = sb("v_st", [P, TB, 4, HD], F32R)
        prob = sb("prob", [P, UNITS, T])
        pt_hi, pt_lo = sb("pt_hi", [P, 2, T], F32R), sb("pt_lo", [P, 2, T], F32R)
        o_tmp, o32 = sb("o_tmp", [P, T]), sb("o32", [P, T])
        o_hi, o_lo = sb("o_hi", [P, T], F32R), sb("o_lo", [P, T], F32R)
        mask_u8 = sb("mask_u8", [P, T], U8)
        mask_add = sb("mask_add", [P, T])
        ident = sb("ident", [P, P])
        nmax, rsum, rinv = sb("nmax", [P, UNITS]), sb("rsum", [P, UNITS]), sb("rinv", [P, UNITS])
        bn = sb("bn", [P, TB, 2, 6])
        mv = sb("mv", [P, TB, 2])
        nmean, vpe, rstd, nhalf = (sb(n, [P, TB]) for n in ("nmean", "vpe", "rstd", "nhalf"))
        gam, bet = sb("gam", [P, KT]), sb("bet", [P, KT])
        gate_in, tg = sb("gate_in", [P, 1]), sb("tg", [P, 1])

        so = [bank("so0"), bank("so1")]
        pt = [bank("pt0"), bank("pt1")]
        pv = [bank("pv0"), bank("pv1")]
        po = so + pv
        pj = [bank("pj0"), bank("pj1")]

        const_ld, x_ld, ctx_ld, mask_ld = sem("const_ld"), sem("x_ld"), sem("ctx_ld"), sem("mask_ld")
        w_ld = [sem("w_ld0"), sem("w_ld1")]
        y_st, kx_done = sem("y_st"), sem("kx_done")
        so_read = sem("so_read")
        pl_done = sem("pl_done")
        rinv_done, ql_done, kl_done, vl_done = sem("rinv_done"), sem("ql_done"), sem("kl_done"), sem("vl_done")
        oadd_done, ol_done = sem("oadd_done"), sem("ol_done")
        mask_done, bn_done, stat_done = sem("mask_done"), sem("bn_done"), sem("stat_done")
        xlv_done, alv_done = sem("xlv_done"), sem("alv_done")
        tg_done, exp_done, vt_done, vh_done = sem("tg_done"), sem("exp_done"), sem("vt_done"), sem("vh_done")
        qh_done, kh_done, ph_done = sem("qh_done"), sem("kh_done"), sem("ph_done")
        otmp_done, oh_done, whi_done = sem("otmp_done"), sem("oh_done"), sem("whi_done")
        xh_done, at_done, ah_done = sem("xh_done"), sem("at_done"), sem("ah_done")
        ident_done, nhalf_done, scale_done, wlo_done = (
            sem("ident_done"), sem("nhalf_done"), sem("scale_done"), sem("wlo_done"))
        rstd_done, z_done, xlp_done, alp_done = sem("rstd_done"), sem("z_done"), sem("xlp_done"), sem("alp_done")
        s_done, vtr_done, t_done, pv_done, op_done = (
            sem("s_done"), sem("vtr_done"), sem("t_done"), sem("pv_done"), sem("op_done"))
        q_done, k_done, v_done, ct_done = sem("q_done"), sem("k_done"), sem("v_done"), sem("ct_done")

        def f32(ap):
            return ap.bitcast(F32)

        def at(i):
            return cx[:, :, i * P:(i + 1) * P]

        def blocks(ap):
            return ap.rearrange("p (s t) -> p s t", s=TB)

        lo_half, hi_half = slice(0, HD), slice(HD, P)

        def w_number(kind, k):
            return 4 * k + {WV: 5, WO: 6, WQ: 7, WK: 8}[kind]

        def w_slot(kind):
            return 1 if kind in (WV, WQ) else 0

        def w_loaded(kind, k):
            return 16 * (2 * k + {WV: 3, WQ: 4, WO: 4, WK: 5}[kind])

        block = es.enter_context(nc.Block())

        def run_loops(eng, body):
            with eng.Fori(0, B - 1) as b:
                with eng.Fori(0, PAIRS - 2) as j:
                    body(b * PAIRS + j, b, j, "plain")
                body(b * PAIRS + (PAIRS - 2), b, PAIRS - 2, "prepare")
                body(b * PAIRS + (PAIRS - 1), b, PAIRS - 1, "switch")
            with eng.Fori(0, PAIRS - 2) as j:
                body(j + (B - 1) * PAIRS, B - 1, j, "plain")
            body(LAST - 1, B - 1, PAIRS - 2, "plain")
            body(LAST, B - 1, PAIRS - 1, "last")

        @block.sync
        def _(sp):
            def load_w(kind, j, k):
                m, s = w_number(kind, k), w_slot(kind)
                sp.wait_ge(wlo_done, m - 1)
                sp.nop(nofuse=True)
                sp.dma_start(w_raw[:, s], wts[kind][bass.ds(j, 1)].rearrange("a p n -> p (a n)")).then_inc(w_ld[s], 16)

            def load_x(b, parity):
                sp.dma_start(xy[:, bass.ds(parity, 1)].rearrange("p a k t -> p (a k t)"),
                             xT[bass.ds(b, 1)].rearrange("a p n -> p (a n)")).then_inc(x_ld, 16)

            def load_ctx(b):
                sp.dma_start(cx[:], ctx[bass.ds(b, 1)].rearrange("a (s p) d -> p (a s) d", p=P)).then_inc(ctx_ld, 16)

            def load_mask(b):
                sp.dma_start(mask_u8[:], mask[bass.ds(b, 1), :].to_broadcast((P, T))).then_inc(mask_ld, 16)

            sp.sem_inc(y_st, 16)
            load_ctx(0)
            sp.dma_start(w_raw[:, 0], wts[WQ][0]).then_inc(w_ld[0], 16)
            load_x(0, 0)
            sp.dma_start(w_raw[:, 1], wts[WK][0]).then_inc(w_ld[1], 16)
            load_mask(0)
            sp.dma_start(gam[:], gamma).then_inc(const_ld, 16)
            sp.dma_start(bet[:], beta).then_inc(const_ld, 16)
            sp.dma_start(gate_in[:], gate.to_broadcast((P, 1))).then_inc(const_ld, 16)
            for m, (kind, j) in enumerate([(WV, 0), (WQ, 1), (WK, 1)], 2):
                sp.wait_ge(wlo_done, m - 1)
                sp.dma_start(w_raw[:, m % 2], wts[kind][j]).then_inc(w_ld[m % 2], 16)

            def next_inputs(b):
                sp.wait_ge(y_st, b * 16 + 16)
                sp.nop(nofuse=True)
                load_x(b + 1, (b + 1) % 2)
                sp.wait_ge(alv_done, b * BY_V + BY_V)
                sp.wait_ge(alp_done, b * BY_V + BY_V)
                sp.nop(nofuse=True)
                load_ctx(b + 1)
                sp.wait_ge(mask_done, b * 2 + 2)
                sp.nop(nofuse=True)
                load_mask(b + 1)

            def first_weights(j, k):
                load_w(WV, (j + 1) % PAIRS if isinstance(j, int) else j + 1, k)
                load_w(WO, j, k)

            def second_weights(j, k):
                load_w(WQ, (j + 2) % PAIRS if isinstance(j, int) else j + 2, k)
                load_w(WK, (j + 2) % PAIRS if isinstance(j, int) else j + 2, k)
                swap_k(k)

            def swap_k(k):
                sp.wait_ge(kl_done, k * 2 + 4)
                for h, (src, dst) in enumerate(((lo_half, hi_half), (hi_half, lo_half))):
                    for order in range(2):
                        sp.dma_start(f32(k_st[dst, h, order]), f32(k_st[src, h, 1 - order])).then_inc(kx_done, 16)

            def store_y(b):
                sp.wait_ge(so_read, (b + 1) * (16 * PAIRS) + 4)
                sp.nop(nofuse=True)
                sp.dma_start(yT[bass.ds(b, 1)].rearrange("a p n -> p (a n)"),
                             xy[:, bass.ds(b % 2, 1)].rearrange("p a k t -> p (a k t)")).then_inc(y_st, 16)

            def batch(b, more):
                k = b * PAIRS
                with sp.Fori(1, PAIRS - 2) as j:
                    first_weights(j, k + j)
                    second_weights(j, k + j)
                for j in (PAIRS - 2, PAIRS - 1):
                    first_weights(j, k + j)
                    second_weights(j, k + j)
                first_weights(0, k + PAIRS)
                store_y(b)
                second_weights(0, k + PAIRS)
                if more:
                    next_inputs(b + 1)

            swap_k(-1)
            first_weights(0, 0)
            second_weights(0, 0)
            next_inputs(0)
            with sp.Fori(0, B - 2) as b:
                batch(b, True)
            batch(B - 2, False)
            with sp.Fori(1, PAIRS - 2) as j:
                first_weights(j, j + (B - 1) * PAIRS)
                second_weights(j, j + (B - 1) * PAIRS)
            first_weights(PAIRS - 2, LAST - 1)
            second_weights(PAIRS - 2, LAST - 1)
            load_w(WO, PAIRS - 1, LAST)
            store_y(B - 1)
            sp.wait_ge(y_st, 16 * B + 16)

        @block.tensor
        def _(pe):
            def scores(k, u):
                h, t = divmod(u, TB)
                if u == 0:
                    pe.wait_ge(ql_done, k * 2 + 2)
                    pe.wait_ge(kx_done, k * 64 + 64)
                pe.wait_ge(so_read, k * 16 + (u + 1 if u < 2 else u + 3))
                for order in range(2):
                    mm = pe.matmul(so[u % 2][:], q_st[:, h, t * P:(t + 1) * P], k_st[:, h, order],
                                   start=order == 0, stop=order == 1)
                mm.then_inc(s_done, 1)

            def turn_v(k):
                pe.wait_ge(vt_done, k + 1)
                pe.wait_ge(ident_done, 2)
                for s in range(TB):
                    mm = pe.transpose(pj[0][:, s * P:(s + 1) * P], vt[:, s * P:(s + 1) * P], ident[:])
                mm.then_inc(vtr_done, 1)

            def turn_p(k, u, kind):
                h, s = divmod(u, TB)
                if s == 0:
                    pe.wait_ge(scale_done, k * UNITS + TB * (h + 1))
                pe.wait_ge(pl_done, k * UNITS + (u + 1))
                for t in range(TB):
                    mm = pe.transpose(pt[u % 2][:, t * P:(t + 1) * P], prob[:, h * TB + t, s * P:(s + 1) * P],
                                      ident[:])
                mm.then_inc(t_done, 1)

            def values(k, u):
                h, s = divmod(u, TB)
                if s == 0:
                    pe.wait_ge(vl_done, k + 1)
                pe.wait_ge(pl_done, k * UNITS + (u + 3))
                w = v_st[:, s, 2 * h:2 * h + 2].rearrange("p a d -> p (a d)")
                pe.matmul(pv[h][:], w, pt_hi[:, u % 2], start=s == 0, stop=False)
                pe.matmul(pv[h][:], w, pt_lo[:, u % 2], start=False, stop=s == TB - 1).then_inc(pv_done, 1)

            def partial_out(k, n, kind, stream):
                if n == 0:
                    pe.wait_ge(oh_done, k + 1)
                    pe.wait_ge(wlo_done, w_number(WO, k) + (0 if kind == "last" else 1))
                if n < 2:
                    pe.wait_ge(so_read, k * 16 + (UNITS + n + 3))
                if n >= 4:
                    pe.wait_ge(so_read, k * 16 + (UNITS + n + 1))
                cols = slice(n * P, (n + 1) * P)
                pe.matmul(po[n % 4][:], w_hi[:, WO, cols], o_hi[:], start=True, stop=False)
                pe.matmul(po[n % 4][:], w_lo[:, WO, cols], o_hi[:], start=False, stop=False)
                if n == 0:
                    take(stream, FILL_O[0])
                    pe.wait_ge(ol_done, k + 1)
                pe.matmul(po[n % 4][:], w_hi[:, WO, cols], o_lo[:], start=False, stop=True).then_inc(op_done, 1)
                if n:
                    take(stream, FILL_O[n])

            def projections(k, b, kind):
                first = isinstance(k, int) and k == -1
                for w, dst, done, s_hi, s_lo in ((WQ, pj[1], q_done, x_hi, x_lo), (WK, pj[0], k_done, a_hi, a_lo),
                                                 (WV, pj[1], v_done, a_hi, a_lo)):
                    if first:
                        pe.wait_ge(wlo_done, w + 1)
                        if w == WV:
                            pe.wait_ge(ql_done, 2)
                    elif w == WQ:
                        pe.wait_ge(wlo_done, k * 4 + 4)
                        pe.wait_ge(vt_done, k + 1)
                    elif w == WK:
                        pe.wait_ge(wlo_done, k * 4 + 5)
                        pe.wait_ge(vl_done, k + 1)
                    else:
                        pe.wait_ge(wlo_done, k * 4 + 6)
                        pe.wait_ge(ql_done, k * 2 + 4)
                    for i in range(KT):
                        if kind == "switch" and w != WV:
                            by_v, by_p = (xlv_done, xlp_done) if w == WQ else (alv_done, alp_done)
                            pe.wait_ge(by_v if i < BY_V else by_p, b * BY_V + (BY_V + i % BY_V + 1))
                        cols = slice(i * P, (i + 1) * P)
                        pe.matmul(dst[:], w_hi[:, w, cols], s_hi[:, i], start=i == 0, stop=False)
                        yield
                        pe.matmul(dst[:], w_hi[:, w, cols], s_lo[:, i], start=False, stop=False)
                        yield
                        mm = pe.matmul(dst[:], w_lo[:, w, cols], s_hi[:, i], start=False, stop=i == KT - 1)
                        if i == KT - 1:
                            mm.then_inc(done, 1)
                        yield

            def turn_ctx(k, b, i):
                if i == 0:
                    pe.wait_ge(z_done, b * TB + 2 * TB)
                if i < 2 and not (isinstance(k, int) and k == -1):
                    pe.wait_ge(pl_done, k * UNITS + (UNITS + 2))
                if i >= 2:
                    pe.wait_ge(at_done, b * KT + (KT + i - 1))
                for s in range(TB):
                    mm = pe.transpose(pt[i % 2][:, s * P:(s + 1) * P], cx[:, s, i * P:(i + 1) * P], ident[:])
                mm.then_inc(ct_done, 1)

            def take(stream, n):
                for _ in range(n):
                    next(stream, None)

            def body(k, b, j, kind):
                stream = iter(()) if kind == "last" else projections(k, b, kind)
                for u in range(UNITS):
                    scores(k, u)
                    if u == 0:
                        turn_v(k)
                    take(stream, FILL_S[u])
                if kind == "switch":
                    pe.wait_ge(at_done, b * KT + 2 * KT)
                for u in range(UNITS):
                    turn_p(k, u, kind)
                    take(stream, FILL_T[u])
                    if u:
                        values(k, u - 1)
                take(stream, FILL_GAP[0])
                values(k, UNITS - 1)
                take(stream, FILL_GAP[1])
                for n in range(KT):
                    partial_out(k, n, kind, stream)
                    if kind == "prepare":
                        turn_ctx(k, b, n)

            stream = projections(-1, -1, "switch")
            take(stream, 3 * KT)
            pe.wait_ge(ident_done, 2)
            for i in range(KT):
                turn_ctx(-1, -1, i)
            take(stream, 6 * KT)
            run_loops(pe, body)

        @block.scalar
        def _(act):
            def split_w(kind, k, number=None):
                s = w_slot(kind)
                act.wait_ge(w_ld[s], w_loaded(kind, k))
                if kind == WQ:
                    act.wait_ge(q_done, k + 2)
                if kind == WK:
                    act.wait_ge(k_done, k + 2)
                act.copy(w_hi[:, kind], w_raw[:, s]).then_inc(whi_done, 1)

            def split_wo(k, half):
                s, cols = w_slot(WO), slice(half * T, (half + 1) * T)
                if half == 0:
                    act.wait_ge(w_ld[s], w_loaded(WO, k))
                op = act.copy(w_hi[:, WO, cols], w_raw[:, s, cols])
                if half:
                    op.then_inc(whi_done, 1)

            def copy_vt(k):
                act.wait_ge(v_done, k + 1)
                act.copy(vt[:], pj[1][:]).then_inc(vt_done, 1)

            def exp(k, u):
                act.wait_ge(so_read, k * 16 + (u + 5))
                act.activation(prob[:, u], prob[:, u], ACT.Exp, bias=nmax[:, u:u + 1], scale=-1.0,
                               accum_out=rsum[:, u:u + 1]).then_inc(exp_done, 1)

            def v_high(k):
                act.wait_ge(vtr_done, k + 1)
                act.copy(v_st[:, :, 0:4:3], pj[0][:].rearrange("p (s h d) -> p s h d", s=TB, h=2)).then_inc(vh_done, 1)

            def q_high(k, h):
                if h == 0:
                    act.wait_ge(q_done, k + 2)
                half = hi_half if h else lo_half
                act.copy(q_st[half, h], pj[1][half]).then_inc(qh_done, 1)

            def k_high(k, h):
                if h == 0:
                    act.wait_ge(k_done, k + 2)
                half = hi_half if h else lo_half
                act.copy(k_st[half, h, 0], pj[0][half]).then_inc(kh_done, 1)

            def p_high(k, u):
                act.wait_ge(t_done, k * UNITS + (u + 1))
                act.copy(pt_hi[:, u % 2], pt[u % 2][:]).then_inc(ph_done, 1)

            def o_move(k, h):
                act.wait_ge(pv_done, k * UNITS + TB * (h + 1))
                src, dst = (lo_half, hi_half) if h else (hi_half, lo_half)
                act.copy(o_tmp[dst], pv[h][src]).then_inc(otmp_done, 1)

            def o_high(k):
                act.wait_ge(oadd_done, k * 2 + 2)
                act.copy(o_hi[:], o32[:]).then_inc(oh_done, 1)

            def x_high(k, b, i, parity):
                if i == 0:
                    act.wait_ge(x_ld, b * 16 + 32)
                    if not isinstance(k, int):
                        act.wait_ge(q_done, k + 2)
                    act.nop(nofuse=True)
                act.copy(x_hi[:, i], xy[:, bass.ds(parity, 1), i].rearrange("p a t -> p (a t)")).then_inc(xh_done, 1)

            def a_float(b, i):
                act.wait_ge(ct_done, b * KT + (KT + i + 1))
                act.activation(at(i), pt[i % 2][:].rearrange("p (s t) -> p s t", s=TB), ACT.Identity,
                               bias=bet[:, i:i + 1], scale=gam[:, i:i + 1]).then_inc(at_done, 1)

            def a_high(b, i):
                act.wait_ge(at_done, b * KT + (KT + i + 1))
                act.copy(blocks(a_hi[:, i]), at(i)).then_inc(ah_done, 1)

            def body(k, b, j, kind):
                last = kind == "last"
                copy_vt(k)
                v_high(k)
                for u in range(UNITS):
                    exp(k, u)
                    if kind == "switch":
                        if u < 6:
                            a_high(b, u)
                    elif u == 3 and not last:
                        split_w(WV, k)
                    if u == 6 and not last:
                        q_high(k, 0)
                for u in range(UNITS):
                    p_high(k, u)
                    if u == 1 and not last:
                        q_high(k, 1)
                    if kind == "switch" and u < 2:
                        a_high(b, 6 + u)
                    if kind == "switch" and u == 2:
                        split_w(WV, k)
                    if u in (3, 4):
                        split_wo(k, u - 3)
                    if u == UNITS - 1 and not last:
                        for h in range(2):
                            k_high(k, h)
                    if u == 5:
                        o_move(k, 0)
                    if kind == "prepare":
                        x_high(k, b, u, (b + 1) % 2)
                o_move(k, 1)
                o_high(k)
                if last:
                    return
                if kind == "prepare":
                    for i in range(2):
                        a_float(b, i)
                split_w(WQ, k)
                if kind == "prepare":
                    for i in range(2, KT):
                        a_float(b, i)
                split_w(WK, k)

            act.wait_ge(w_ld[0], 16)
            act.copy(w_hi[:, WQ], w_raw[:, 0]).then_inc(whi_done, 1)
            for i in range(KT):
                x_high(-1, -1, i, 0)
            act.wait_ge(w_ld[1], 16)
            act.copy(w_hi[:, WK], w_raw[:, 1]).then_inc(whi_done, 1)
            act.wait_ge(const_ld, 48)
            act.activation(tg[:], gate_in[:], ACT.Tanh).then_inc(tg_done, 1)
            for i in range(KT):
                a_float(-1, i)
            for i in range(KT):
                a_high(-1, i)
            act.wait_ge(w_ld[0], 32)
            act.copy(w_hi[:, WV], w_raw[:, 0]).then_inc(whi_done, 1)
            q_high(-1, 0)
            q_high(-1, 1)
            act.wait_ge(w_ld[1], 32)
            act.copy(w_hi[:, WQ], w_raw[:, 1]).then_inc(whi_done, 1)
            for h in range(2):
                k_high(-1, h)
            act.wait_ge(w_ld[0], 48)
            act.copy(w_hi[:, WK], w_raw[:, 0]).then_inc(whi_done, 1)
            run_loops(act, body)

        @block.vector
        def _(dve):
            def row_max(k, u):
                dve.wait_ge(s_done, k * UNITS + (u + 1))
                dve.nop(nofuse=True)
                dve.wait_ge(mask_done, 2)
                dve.tensor_tensor_reduce(prob[:, u], so[u % 2][:], mask_add[:], -SCALE, BIG, ALU.add, ALU.min,
                                         nmax[:, u:u + 1]).then_inc(so_read, 1)

            def inverse_sums(k, i):
                dve.wait_ge(exp_done, k * UNITS + 2 * (i + 1))
                dve.reciprocal(rinv[:, 2 * i:2 * i + 2], rsum[:, 2 * i:2 * i + 2]).then_inc(rinv_done, 1)

            def v_low(k):
                dve.wait_ge(vh_done, k + 1)
                dve.tensor_tensor(v_st[:, :, 1:3], pj[0][:].rearrange("p (s h d) -> p s h d", s=TB, h=2),
                                  f32(v_st[:, :, 0:4:3]), ALU.subtract).then_inc(vl_done, 1)

            def q_low(k, h):
                dve.wait_ge(qh_done, k * 2 + (3 + h))
                src, dst = (hi_half, lo_half) if h else (lo_half, hi_half)
                dve.tensor_tensor(q_st[dst, h], pj[1][src], f32(q_st[src, h]), ALU.subtract).then_inc(ql_done, 1)

            def k_low(k, h):
                dve.wait_ge(kh_done, k * 2 + (3 + h))
                half = hi_half if h else lo_half
                dve.tensor_tensor(k_st[half, h, 1], pj[0][half], f32(k_st[half, h, 0]),
                                  ALU.subtract).then_inc(kl_done, 1)

            def p_low(k, u):
                dve.wait_ge(ph_done, k * UNITS + (u + 1))
                dve.tensor_tensor(pt_lo[:, u % 2], pt[u % 2][:], f32(pt_hi[:, u % 2]),
                                  ALU.subtract).then_inc(pl_done, 1)

            def o_add(k, h):
                dve.wait_ge(otmp_done, k * 2 + (h + 1))
                rows = hi_half if h else lo_half
                dve.tensor_tensor(o32[rows], pv[h][rows], o_tmp[rows], ALU.add).then_inc(oadd_done, 1)

            def o_low(k):
                dve.wait_ge(oh_done, k + 1)
                dve.tensor_tensor(o_lo[:], o32[:], f32(o_hi[:]), ALU.subtract).then_inc(ol_done, 1)

            def accumulate(k, n, parity):
                dve.wait_ge(op_done, k * KT + (n + 1))
                y = xy[:, bass.ds(parity, 1), n].rearrange("p a t -> p (a t)")
                dve.scalar_tensor_tensor(out=y, in0=po[n % 4][:], scalar=tg[:], in1=y,
                                         op0=ALU.mult, op1=ALU.add).then_inc(so_read, 1)

            def x_low(b, i, parity):
                dve.wait_ge(xh_done, b * KT + (KT + i + 1))
                dve.tensor_tensor(x_lo[:, i], xy[:, bass.ds(parity, 1), i].rearrange("p a t -> p (a t)"), f32(x_hi[:, i]),
                                  ALU.subtract).then_inc(xlv_done, 1)

            def a_low(b, i):
                dve.wait_ge(ah_done, b * KT + (KT + i + 1))
                dve.tensor_tensor(blocks(a_lo[:, i]), at(i), f32(blocks(a_hi[:, i])), ALU.subtract).then_inc(alv_done, 1)

            def build_mask(b):
                dve.wait_ge(mask_ld, b * 16 + 32)
                dve.tensor_scalar(mask_add[:], mask_u8[:], -1.0, BIG, ALU.add, ALU.mult).then_inc(mask_done, 1)
                dve.wait_ge(mask_done, b * 2 + 3)
                dve.tensor_scalar(mask_add[:], mask_add[:], BIG, None, ALU.mult).then_inc(mask_done, 1)
                dve.wait_ge(mask_done, b * 2 + 4)

            def row_stats(b, i):
                s, half = divmod(i, 2)
                if i == 0:
                    dve.wait_ge(ctx_ld, b * 16 + 32)
                dve.bn_stats(bn[:, s, half], cx[:, s, half * T:(half + 1) * T]).then_inc(bn_done, 1)

            def row_moments(b):
                dve.wait_ge(bn_done, b * 3 * TB + 5 * TB)
                dve.nop(nofuse=True)
                for s in range(TB):
                    dve.bn_aggr(mv[:, s], bn[:, s].rearrange("p a c -> p (a c)")).then_inc(bn_done, 1)
                dve.wait_ge(bn_done, b * 3 * TB + 6 * TB)
                dve.tensor_scalar(nmean[:], mv[:, :, 0], -1.0, None, ALU.mult).then_inc(stat_done, 1)
                dve.tensor_scalar(vpe[:], mv[:, :, 1], EPS, None, ALU.add).then_inc(stat_done, 1)

            def body(k, b, j, kind):
                last = kind == "last"
                parity = b % 2
                for u in range(UNITS):
                    row_max(k, u)
                    if u == 1:
                        v_low(k)
                    if u in (3, 5, 7):
                        inverse_sums(k, (u - 3) // 2)
                    if kind == "prepare":
                        row_stats(b, u)
                    if kind == "switch" and 2 <= u < 2 + BY_V:
                        a_low(b, u - 2)
                if not last:
                    q_low(k, 0)
                inverse_sums(k, 3)
                if kind == "prepare":
                    row_moments(b)
                for u in range(UNITS):
                    p_low(k, u)
                    if u == 1 and not last:
                        q_low(k, 1)
                    if u == 5:
                        o_add(k, 0)
                    if kind == "switch" and u == 4:
                        build_mask(b)
                    if kind == "prepare" and u >= UNITS - BY_V:
                        x_low(b, u - (UNITS - BY_V), (b + 1) % 2)
                if not last:
                    k_low(k, 0)
                    k_low(k, 1)
                o_add(k, 1)
                o_low(k)
                for n in range(KT):
                    accumulate(k, n, parity)

            for i, s in enumerate((pl_done, pl_done, so_read, so_read, so_read, so_read)):
                dve.memset(nmax[:, i:i + 1], 0.0).then_inc(s, 1)
            build_mask(-1)
            for i in range(2 * TB):
                row_stats(-1, i)
            row_moments(-1)
            for i in range(BY_V):
                x_low(-1, i, 0)
            dve.wait_ge(tg_done, 1)
            for i in range(BY_V):
                a_low(-1, i)
            q_low(-1, 0)
            q_low(-1, 1)
            for h in range(2):
                k_low(-1, h)
            run_loops(dve, body)

        @block.gpsimd
        def _(pool):
            def scale_rows(k, u):
                if u % 2 == 0:
                    pool.wait_ge(rinv_done, k * 4 + (u // 2 + 1))
                    pool.nop(nofuse=True)
                pool.tensor_scalar(prob[:, u], prob[:, u], rinv[:, u:u + 1], 1.0, ALU.mult,
                                   ALU.mult).then_inc(scale_done, 1)

            def split_w(kind, k, less=0):
                pool.wait_ge(whi_done, w_number(kind, k) + (1 - less))
                pool.tensor_tensor(w_lo[:, kind], w_raw[:, w_slot(kind)], f32(w_hi[:, kind]),
                                   ALU.subtract).then_inc(wlo_done, 1)

            def norm_rows(b):
                pool.wait_ge(stat_done, b * 2 + 4)
                pool.tensor_tensor(rstd[:], vpe[:], nhalf[:], ALU.pow).then_inc(rstd_done, 1)
                pool.wait_ge(rstd_done, b + 2)
                pool.nop(nofuse=True)
                for s in range(TB):
                    pool.tensor_scalar(cx[:, s], cx[:, s], nmean[:, s:s + 1], rstd[:, s:s + 1], ALU.add,
                                       ALU.mult).then_inc(z_done, 1)

            def x_low(b, i, parity):
                pool.wait_ge(xh_done, b * KT + (KT + i + 1))
                pool.nop(nofuse=True)
                pool.tensor_tensor(x_lo[:, i], xy[:, bass.ds(parity, 1), i].rearrange("p a t -> p (a t)"),
                                   f32(x_hi[:, i]), ALU.subtract).then_inc(xlp_done, 1)

            def a_low(b, i):
                pool.wait_ge(ah_done, b * KT + (KT + i + 1))
                pool.tensor_tensor(blocks(a_lo[:, i]), at(i), f32(blocks(a_hi[:, i])),
                                   ALU.subtract).then_inc(alp_done, 1)

            def body(k, b, j, kind):
                for u in range(UNITS):
                    scale_rows(k, u)
                    if kind == "switch" and u in (3, 5, 7):
                        a_low(b, BY_V + (u - 3) // 2)
                if kind == "last":
                    return split_w(WO, k, less=1)
                if kind == "prepare":
                    norm_rows(b)
                if kind == "switch":
                    a_low(b, KT - 1)
                split_w(WV, k)
                split_w(WO, k)
                if kind == "prepare":
                    for i in range(BY_V, KT):
                        x_low(b, i, (b + 1) % 2)
                split_w(WQ, k)
                split_w(WK, k)

            pool.memset(ident[:], 0.0).then_inc(ident_done, 1)
            pool.memset(nhalf[:], -0.5).then_inc(nhalf_done, 1)
            pool.wait_ge(ident_done, 1)
            pool.affine_select(out=ident[:], in_=ident[:], compare_op=ALU.not_equal, fill=1.0, base=0,
                               pattern=[[-1, P]], channel_multiplier=1).then_inc(ident_done, 1)
            pool.wait_ge(nhalf_done, 1)

            def split_first(m, kind):
                pool.wait_ge(whi_done, m + 1)
                pool.tensor_tensor(w_lo[:, kind], w_raw[:, m % 2], f32(w_hi[:, kind]),
                                   ALU.subtract).then_inc(wlo_done, 1)

            split_first(0, WQ)
            for i in range(BY_V, KT):
                x_low(-1, i, 0)
            norm_rows(-1)
            split_first(1, WK)
            for i in range(BY_V, KT):
                a_low(-1, i)
            for m, kind in ((2, WV), (3, WQ), (4, WK)):
                split_first(m, kind)
            run_loops(pool, body)


def kernel(**inputs):
    import concourse.bacc as bacc
    from concourse.bass_utils import run_bass_kernel_spmd

    def arr(name):
        return np.asarray(inputs[name])

    def lay(a):
        return np.ascontiguousarray(a)

    def projection(w):
        return lay(w.reshape(PAIRS, P, KT, P).transpose(0, 3, 2, 1)).reshape(PAIRS, P, D)

    arrays = {
        "xT": lay(arr("x").reshape(B, T, KT, P).transpose(0, 3, 2, 1)).reshape(B, P, KT * T),
        "ctx": lay(arr("ctx_2048")),
        "mask": lay(arr("mask_BxS2_bf1")).view(np.uint8),
        "wq": projection(arr("L0_xattn_Wq")),
        "wk": projection(arr("L0_xattn_Wk")),
        "wv": projection(arr("L0_xattn_Wv")),
        "wo": lay(arr("L0_xattn_Wo").T).reshape(PAIRS, P, D),
        "gamma": lay(arr("L0_xattn_ln_gamma").reshape(KT, P).T),
        "beta": lay(arr("L0_xattn_ln_beta").reshape(KT, P).T),
        "gate": lay(arr("L0_xattn_gate").reshape(1, 1)),
    }
    nc = bacc.Bacc("TRN2", target_bir_lowering=False, num_devices=1)
    t = {n: nc.dram_tensor(f"in_{n}", a.shape, mybir.dt.from_np(a.dtype), kind="ExternalInput").ap()
         for n, a in arrays.items()}
    y = nc.dram_tensor("out_y", (B, P, KT * T), F32, kind="ExternalOutput").ap()
    xattn_kernel(nc, t["xT"], t["ctx"], t["mask"], [t["wq"], t["wk"], t["wv"], t["wo"]],
                 t["gamma"], t["beta"], t["gate"], y)
    r = run_bass_kernel_spmd(nc, [{f"in_{n}": a for n, a in arrays.items()}], core_ids=[0])
    out = np.asarray(r.results[0]["out_y"]).reshape(B, P, KT, T).transpose(0, 3, 2, 1)
    return np.ascontiguousarray(out).reshape(B, T, D)
```

```python
from contextlib import ExitStack

import numpy as np

import concourse.bass as bass
from concourse import mybir

F32 = mybir.dt.float32
F32R = mybir.dt.float32r
U8 = mybir.dt.uint8
ACT = mybir.ActivationFunctionType
ALU = mybir.AluOpType

P = 128
B, T, D = 8, 512, 1024
HD = 64
KT = D // P
PAIRS = D // P
TB = T // P
UNITS = 2 * TB
BY_V = KT // 2
SCALE = HD ** -0.5
EPS = 1e-5
BIG = 3.0e38
WQ, WK, WV, WO = range(4)
LAST = B * PAIRS - 1
FILL_S = (0, 4, 4, 4, 4, 4, 5, 5)
FILL_T = (4, 2, 2, 2, 2, 2, 2, 2)
FILL_GAP = (4, 12)
FILL_O = (1, 1, 1, 1, 1, 1, 2, 0)
assert sum(FILL_S) + sum(FILL_T) + sum(FILL_GAP) + sum(FILL_O) == 3 * 3 * KT


def xattn_kernel(nc, xT, ctx, mask, wts, gamma, beta, gate, yT):
    es = ExitStack()
    with es:
        def sb(name, shape, dt=F32):
            return es.enter_context(nc.sbuf_tensor(name, shape, dt))

        def bank(name):
            return es.enter_context(nc.psum_tensor(name, [P, T], F32))

        def sem(name):
            return es.enter_context(nc.semaphore(name))

        xy = sb("xy", [P, 2, KT, T])
        cx = sb("cx", [P, TB, D])
        x_hi, x_lo = sb("x_hi", [P, KT, T], F32R), sb("x_lo", [P, KT, T], F32R)
        a_hi, a_lo = sb("a_hi", [P, KT, T], F32R), sb("a_lo", [P, KT, T], F32R)
        w_raw = sb("w_raw", [P, 2, D])
        w_hi, w_lo = sb("w_hi", [P, 4, D], F32R), sb("w_lo", [P, 4, D], F32R)
        q_st = sb("q_st", [P, 2, T], F32R)
        k_st = sb("k_st", [P, 2, 2, T], F32R)
        vt = sb("vt", [P, T])
        v_st = sb("v_st", [P, TB, 4, HD], F32R)
        prob = sb("prob", [P, UNITS, T])
        pt_hi, pt_lo = sb("pt_hi", [P, 2, T], F32R), sb("pt_lo", [P, 2, T], F32R)
        o_tmp, o32 = sb("o_tmp", [P, T]), sb("o32", [P, T])
        o_hi, o_lo = sb("o_hi", [P, T], F32R), sb("o_lo", [P, T], F32R)
        mask_u8 = sb("mask_u8", [P, T], U8)
        mask_add = sb("mask_add", [P, T])
        ident = sb("ident", [P, P])
        nmax, rsum, rinv = sb("nmax", [P, UNITS]), sb("rsum", [P, UNITS]), sb("rinv", [P, UNITS])
        bn = sb("bn", [P, TB, 2, 6])
        mv = sb("mv", [P, TB, 2])
        nmean, vpe, rstd, nhalf = (sb(n, [P, TB]) for n in ("nmean", "vpe", "rstd", "nhalf"))
        gam, bet = sb("gam", [P, KT]), sb("bet", [P, KT])
        gate_in, tg = sb("gate_in", [P, 1]), sb("tg", [P, 1])

        so = [bank("so0"), bank("so1")]
        pt = [bank("pt0"), bank("pt1")]
        pv = [bank("pv0"), bank("pv1")]
        po = so + pv
        pj = [bank("pj0"), bank("pj1")]

        const_ld, x_ld, ctx_ld, mask_ld = sem("const_ld"), sem("x_ld"), sem("ctx_ld"), sem("mask_ld")
        x_first, ctx_first = ([sem(f"{n}_first{i}") for i in range(4)] for n in ("x", "ctx"))
        w_ld = [sem("w_ld0"), sem("w_ld1")]
        y_st, kx_done = sem("y_st"), sem("kx_done")
        so_read = sem("so_read")
        pl_done = sem("pl_done")
        rinv_done, ql_done, kl_done, vl_done = sem("rinv_done"), sem("ql_done"), sem("kl_done"), sem("vl_done")
        oadd_done, ol_done = sem("oadd_done"), sem("ol_done")
        mask_done, bn_done, stat_done = sem("mask_done"), sem("bn_done"), sem("stat_done")
        xlv_done, alv_done = sem("xlv_done"), sem("alv_done")
        tg_done, exp_done, vt_done, vh_done = sem("tg_done"), sem("exp_done"), sem("vt_done"), sem("vh_done")
        qh_done, kh_done, ph_done = sem("qh_done"), sem("kh_done"), sem("ph_done")
        otmp_done, oh_done, whi_done = sem("otmp_done"), sem("oh_done"), sem("whi_done")
        xh_done, at_done, ah_done = sem("xh_done"), sem("at_done"), sem("ah_done")
        ident_done, nhalf_done, scale_done, wlo_done = (
            sem("ident_done"), sem("nhalf_done"), sem("scale_done"), sem("wlo_done"))
        rstd_done, z_done, xlp_done, alp_done = sem("rstd_done"), sem("z_done"), sem("xlp_done"), sem("alp_done")
        s_done, vtr_done, t_done, pv_done, op_done = (
            sem("s_done"), sem("vtr_done"), sem("t_done"), sem("pv_done"), sem("op_done"))
        q_done, k_done, v_done, ct_done = sem("q_done"), sem("k_done"), sem("v_done"), sem("ct_done")

        def f32(ap):
            return ap.bitcast(F32)

        def at(i):
            return cx[:, :, i * P:(i + 1) * P]

        def blocks(ap):
            return ap.rearrange("p (s t) -> p s t", s=TB)

        lo_half, hi_half = slice(0, HD), slice(HD, P)

        def w_number(kind, k):
            return 4 * k + {WV: 5, WO: 6, WQ: 7, WK: 8}[kind]

        def w_slot(kind):
            return 1 if kind in (WV, WQ) else 0

        def w_loaded(kind, k):
            return 16 * (2 * k + {WV: 3, WQ: 4, WO: 4, WK: 5}[kind])

        block = es.enter_context(nc.Block())

        def run_loops(eng, body):
            with eng.Fori(0, B - 1) as b:
                with eng.Fori(0, PAIRS - 2) as j:
                    body(b * PAIRS + j, b, j, "plain")
                body(b * PAIRS + (PAIRS - 2), b, PAIRS - 2, "prepare")
                body(b * PAIRS + (PAIRS - 1), b, PAIRS - 1, "switch")
            with eng.Fori(0, PAIRS - 2) as j:
                body(j + (B - 1) * PAIRS, B - 1, j, "plain")
            body(LAST - 1, B - 1, PAIRS - 2, "plain")
            body(LAST, B - 1, PAIRS - 1, "last")

        @block.sync
        def _(sp):
            def load_w(kind, j, k):
                m, s = w_number(kind, k), w_slot(kind)
                sp.wait_ge(wlo_done, m - 1)
                sp.nop(nofuse=True)
                sp.dma_start(w_raw[:, s], wts[kind][bass.ds(j, 1)].rearrange("a p n -> p (a n)")).then_inc(w_ld[s], 16)

            def load_mask(b):
                sp.dma_start(mask_u8[:], mask[bass.ds(b, 1), :].to_broadcast((P, T))).then_inc(mask_ld, 16)

            sp.sem_inc(y_st, 16)
            sp.dma_start(w_raw[:, 0], wts[WQ][0]).then_inc(w_ld[0], 16)
            for s in range(TB):
                sp.dma_start(cx[:, s], ctx[0, s * P:(s + 1) * P]).then_inc(ctx_first[s], 16)
            sp.dma_start(gam[:], gamma).then_inc(const_ld, 16)
            sp.dma_start(bet[:], beta).then_inc(const_ld, 16)
            sp.dma_start(gate_in[:], gate.to_broadcast((P, 1))).then_inc(const_ld, 16)
            load_mask(0)
            for c in range(4):
                sp.dma_start(xy[:, 0, 2 * c:2 * c + 2].rearrange("p k t -> p (k t)"),
                             xT[0, :, c * 2 * T:(c + 1) * 2 * T]).then_inc(x_first[c], 16)
            sp.dma_start(w_raw[:, 1], wts[WK][0]).then_inc(w_ld[1], 16)
            for m, (kind, j) in enumerate([(WV, 0), (WQ, 1), (WK, 1)], 2):
                sp.wait_ge(wlo_done, m - 1)
                sp.dma_start(w_raw[:, m % 2], wts[kind][j]).then_inc(w_ld[m % 2], 16)

            def load_quarter(b, i):
                sp.wait_ge(y_st, b * 16 + 16)
                sp.wait_ge(alv_done, b * BY_V + BY_V)
                sp.wait_ge(alp_done, b * BY_V + BY_V)
                sp.nop(nofuse=True)
                sp.dma_start(xy[:, bass.ds((b + 1) % 2, 1), bass.ds(2 * i, 2)].rearrange("p a k t -> p (a k t)"),
                             xT[bass.ds(b + 1, 1), :, bass.ds(i * 2 * T, 2 * T)].rearrange("a p n -> p (a n)")
                             ).then_inc(x_ld, 16)
                sp.dma_start(cx[:, bass.ds(i, 1)].rearrange("p a d -> p (a d)"),
                             ctx[bass.ds(b + 1, 1), bass.ds(i * P, P)].rearrange("a p d -> p (a d)")
                             ).then_inc(ctx_ld, 16)

            def next_mask(b):
                sp.wait_ge(mask_done, b * 2 + 2)
                sp.nop(nofuse=True)
                load_mask(b + 1)

            def first_weights(j, k):
                load_w(WV, (j + 1) % PAIRS if isinstance(j, int) else j + 1, k)
                load_w(WO, j, k)

            def second_weights(j, k):
                load_w(WQ, (j + 2) % PAIRS if isinstance(j, int) else j + 2, k)
                load_w(WK, (j + 2) % PAIRS if isinstance(j, int) else j + 2, k)
                swap_k(k)

            def swap_k(k):
                sp.wait_ge(kl_done, k * 2 + 4)
                for h, (src, dst) in enumerate(((lo_half, hi_half), (hi_half, lo_half))):
                    for order in range(2):
                        sp.dma_start(f32(k_st[dst, h, order]), f32(k_st[src, h, 1 - order])).then_inc(kx_done, 16)

            def store_y(b):
                sp.wait_ge(so_read, (b + 1) * (16 * PAIRS) + 4)
                sp.nop(nofuse=True)
                sp.dma_start(yT[bass.ds(b, 1)].rearrange("a p n -> p (a n)"),
                             xy[:, bass.ds(b % 2, 1)].rearrange("p a k t -> p (a k t)")).then_inc(y_st, 16)

            def weights(j, k):
                first_weights(j, k)
                second_weights(j, k)

            def batch(b, first=False):
                k = b * PAIRS
                first_weights(0, k)
                if not first:
                    store_y(b - 1)
                second_weights(0, k)
                next_mask(b)
                with sp.Fori(1, 5) as j:
                    weights(j, j + k)
                    load_quarter(b, j - 1)
                for j in range(5, PAIRS):
                    weights(j, k + j)

            swap_k(-1)
            batch(0, first=True)
            with sp.Fori(1, B - 1) as b:
                batch(b)
            first_weights(0, LAST + 1 - PAIRS)
            store_y(B - 2)
            second_weights(0, LAST + 1 - PAIRS)
            with sp.Fori(1, PAIRS - 2) as j:
                weights(j, j + (B - 1) * PAIRS)
            weights(PAIRS - 2, LAST - 1)
            load_w(WO, PAIRS - 1, LAST)
            for n in range(KT):
                sp.wait_ge(so_read, B * (16 * PAIRS) + 4 - KT + n + 1)
                sp.dma_start(yT[B - 1, :, n * T:(n + 1) * T], xy[:, (B - 1) % 2, n]).then_inc(y_st, 16)
            sp.wait_ge(y_st, 16 * B + 16 * KT)

        @block.tensor
        def _(pe):
            def scores(k, u):
                h, t = divmod(u, TB)
                if u == 0:
                    pe.wait_ge(ql_done, k * 2 + 2)
                    pe.wait_ge(kx_done, k * 64 + 64)
                pe.wait_ge(so_read, k * 16 + (u + 1 if u < 2 else u + 3))
                for order in range(2):
                    mm = pe.matmul(so[u % 2][:], q_st[:, h, t * P:(t + 1) * P], k_st[:, h, order],
                                   start=order == 0, stop=order == 1)
                mm.then_inc(s_done, 1)

            def turn_v(k):
                pe.wait_ge(vt_done, k + 1)
                pe.wait_ge(ident_done, 2)
                for s in range(TB):
                    mm = pe.transpose(pj[0][:, s * P:(s + 1) * P], vt[:, s * P:(s + 1) * P], ident[:])
                mm.then_inc(vtr_done, 1)

            def turn_p(k, u, kind):
                h, s = divmod(u, TB)
                if s == 0:
                    pe.wait_ge(scale_done, k * UNITS + TB * (h + 1))
                pe.wait_ge(pl_done, k * UNITS + (u + 1))
                for t in range(TB):
                    mm = pe.transpose(pt[u % 2][:, t * P:(t + 1) * P], prob[:, h * TB + t, s * P:(s + 1) * P],
                                      ident[:])
                mm.then_inc(t_done, 1)

            def values(k, u):
                h, s = divmod(u, TB)
                if s == 0:
                    pe.wait_ge(vl_done, k + 1)
                pe.wait_ge(pl_done, k * UNITS + (u + 3))
                w = v_st[:, s, 2 * h:2 * h + 2].rearrange("p a d -> p (a d)")
                pe.matmul(pv[h][:], w, pt_hi[:, u % 2], start=s == 0, stop=False)
                pe.matmul(pv[h][:], w, pt_lo[:, u % 2], start=False, stop=s == TB - 1).then_inc(pv_done, 1)

            def partial_out(k, n, kind, stream):
                if n == 0:
                    pe.wait_ge(oh_done, k + 1)
                    pe.wait_ge(wlo_done, w_number(WO, k) + (0 if kind == "last" else 1))
                if n < 2:
                    pe.wait_ge(so_read, k * 16 + (UNITS + n + 3))
                if n >= 4:
                    pe.wait_ge(so_read, k * 16 + (UNITS + n + 1))
                cols = slice(n * P, (n + 1) * P)
                pe.matmul(po[n % 4][:], w_hi[:, WO, cols], o_hi[:], start=True, stop=False)
                pe.matmul(po[n % 4][:], w_lo[:, WO, cols], o_hi[:], start=False, stop=False)
                if n == 0:
                    take(stream, FILL_O[0])
                    pe.wait_ge(ol_done, k + 1)
                pe.matmul(po[n % 4][:], w_hi[:, WO, cols], o_lo[:], start=False, stop=True).then_inc(op_done, 1)
                if n:
                    take(stream, FILL_O[n])

            def projections(k, b, kind):
                first = isinstance(k, int) and k == -1
                for w, dst, done, s_hi, s_lo in ((WQ, pj[1], q_done, x_hi, x_lo), (WK, pj[0], k_done, a_hi, a_lo),
                                                 (WV, pj[1], v_done, a_hi, a_lo)):
                    if first:
                        pe.wait_ge(wlo_done, w + 1)
                        if w == WV:
                            pe.wait_ge(ql_done, 2)
                    elif w == WQ:
                        pe.wait_ge(wlo_done, k * 4 + 4)
                        pe.wait_ge(vt_done, k + 1)
                    elif w == WK:
                        pe.wait_ge(wlo_done, k * 4 + 5)
                        pe.wait_ge(vl_done, k + 1)
                    else:
                        pe.wait_ge(wlo_done, k * 4 + 6)
                        pe.wait_ge(ql_done, k * 2 + 4)
                    for i in range(KT):
                        if kind == "switch" and w != WV:
                            by_v, by_p = (xlv_done, xlp_done) if w == WQ else (alv_done, alp_done)
                            pe.wait_ge(by_v if i < BY_V else by_p, b * BY_V + (BY_V + i % BY_V + 1))
                        cols = slice(i * P, (i + 1) * P)
                        pe.matmul(dst[:], w_hi[:, w, cols], s_hi[:, i], start=i == 0, stop=False)
                        yield
                        pe.matmul(dst[:], w_hi[:, w, cols], s_lo[:, i], start=False, stop=False)
                        yield
                        mm = pe.matmul(dst[:], w_lo[:, w, cols], s_hi[:, i], start=False, stop=i == KT - 1)
                        if i == KT - 1:
                            mm.then_inc(done, 1)
                        yield

            def turn_ctx(k, b, i):
                if i == 0:
                    pe.wait_ge(z_done, b * TB + 2 * TB)
                if i < 2 and not (isinstance(k, int) and k == -1):
                    pe.wait_ge(pl_done, k * UNITS + (UNITS + 2))
                if i >= 2:
                    pe.wait_ge(at_done, b * KT + (KT + i - 1))
                for s in range(TB):
                    mm = pe.transpose(pt[i % 2][:, s * P:(s + 1) * P], cx[:, s, i * P:(i + 1) * P], ident[:])
                mm.then_inc(ct_done, 1)

            def take(stream, n):
                for _ in range(n):
                    next(stream, None)

            def body(k, b, j, kind):
                stream = iter(()) if kind == "last" else projections(k, b, kind)
                for u in range(UNITS):
                    scores(k, u)
                    if u == 0:
                        turn_v(k)
                    take(stream, FILL_S[u])
                if kind == "switch":
                    pe.wait_ge(at_done, b * KT + 2 * KT)
                for u in range(UNITS):
                    turn_p(k, u, kind)
                    take(stream, FILL_T[u])
                    if u:
                        values(k, u - 1)
                take(stream, FILL_GAP[0])
                values(k, UNITS - 1)
                take(stream, FILL_GAP[1])
                if kind == "prepare":
                    turn_ctx(k, b, 0)
                    turn_ctx(k, b, 1)
                for n in range(KT):
                    partial_out(k, n, kind, stream)
                    if kind == "prepare" and n + 2 < KT:
                        turn_ctx(k, b, n + 2)

            stream = projections(-1, -1, "switch")
            pe.wait_ge(ident_done, 2)
            for i in range(KT):
                turn_ctx(-1, -1, i)
                take(stream, 3)
            take(stream, 6 * KT)
            run_loops(pe, body)

        @block.scalar
        def _(act):
            def split_w(kind, k, number=None):
                s = w_slot(kind)
                act.wait_ge(w_ld[s], w_loaded(kind, k))
                if kind == WQ:
                    act.wait_ge(q_done, k + 2)
                if kind == WK:
                    act.wait_ge(k_done, k + 2)
                act.copy(w_hi[:, kind], w_raw[:, s]).then_inc(whi_done, 1)

            def split_wo(k, half):
                s, cols = w_slot(WO), slice(half * T, (half + 1) * T)
                if half == 0:
                    act.wait_ge(w_ld[s], w_loaded(WO, k))
                op = act.copy(w_hi[:, WO, cols], w_raw[:, s, cols])
                if half:
                    op.then_inc(whi_done, 1)

            def copy_vt(k):
                act.wait_ge(v_done, k + 1)
                act.copy(vt[:], pj[1][:]).then_inc(vt_done, 1)

            def exp(k, u):
                act.wait_ge(so_read, k * 16 + (u + 5))
                act.activation(prob[:, u], prob[:, u], ACT.Exp, bias=nmax[:, u:u + 1], scale=-1.0,
                               accum_out=rsum[:, u:u + 1]).then_inc(exp_done, 1)

            def v_high(k):
                act.wait_ge(vtr_done, k + 1)
                act.copy(v_st[:, :, 0:4:3], pj[0][:].rearrange("p (s h d) -> p s h d", s=TB, h=2)).then_inc(vh_done, 1)

            def q_high(k, h):
                if h == 0:
                    act.wait_ge(q_done, k + 2)
                half = hi_half if h else lo_half
                act.copy(q_st[half, h], pj[1][half]).then_inc(qh_done, 1)

            def k_high(k, h):
                if h == 0:
                    act.wait_ge(k_done, k + 2)
                half = hi_half if h else lo_half
                act.copy(k_st[half, h, 0], pj[0][half]).then_inc(kh_done, 1)

            def p_high(k, u):
                act.wait_ge(t_done, k * UNITS + (u + 1))
                act.copy(pt_hi[:, u % 2], pt[u % 2][:]).then_inc(ph_done, 1)

            def o_move(k, h):
                act.wait_ge(pv_done, k * UNITS + TB * (h + 1))
                src, dst = (lo_half, hi_half) if h else (hi_half, lo_half)
                act.copy(o_tmp[dst], pv[h][src]).then_inc(otmp_done, 1)

            def o_high(k):
                act.wait_ge(oadd_done, k * 2 + 2)
                act.copy(o_hi[:], o32[:]).then_inc(oh_done, 1)

            def x_high(k, b, i, parity):
                if isinstance(b, int) and b == -1:
                    act.wait_ge(x_first[i // 2], 16)
                elif i == 0:
                    act.wait_ge(x_ld, b * 64 + 64)
                    act.wait_ge(q_done, k + 2)
                    act.nop(nofuse=True)
                act.copy(x_hi[:, i], xy[:, bass.ds(parity, 1), i].rearrange("p a t -> p (a t)")).then_inc(xh_done, 1)

            def a_float(b, i):
                act.wait_ge(ct_done, b * KT + (KT + i + 1))
                act.activation(at(i), pt[i % 2][:].rearrange("p (s t) -> p s t", s=TB), ACT.Identity,
                               bias=bet[:, i:i + 1], scale=gam[:, i:i + 1]).then_inc(at_done, 1)

            def a_high(b, i):
                act.wait_ge(at_done, b * KT + (KT + i + 1))
                act.copy(blocks(a_hi[:, i]), at(i)).then_inc(ah_done, 1)

            def body(k, b, j, kind):
                last = kind == "last"
                copy_vt(k)
                v_high(k)
                for u in range(UNITS):
                    exp(k, u)
                    if kind == "switch":
                        if u < 6:
                            a_high(b, u)
                    elif u == 3 and not last:
                        split_w(WV, k)
                    if u == 6 and not last:
                        q_high(k, 0)
                for u in range(UNITS):
                    p_high(k, u)
                    if u == 1 and not last:
                        q_high(k, 1)
                    if kind == "switch" and u < 2:
                        a_high(b, 6 + u)
                    if kind == "switch" and u == 2:
                        split_w(WV, k)
                    if u in (3, 4):
                        split_wo(k, u - 3)
                    if u == UNITS - 1 and not last and kind != "prepare":
                        for h in range(2):
                            k_high(k, h)
                    if u == 5:
                        o_move(k, 0)
                    if kind == "prepare" and u:
                        x_high(k, b, u - 1, (b + 1) % 2)
                o_move(k, 1)
                o_high(k)
                if last:
                    return
                if kind == "prepare":
                    a_float(b, 0)
                    a_float(b, 1)
                    k_high(k, 0)
                    k_high(k, 1)
                    a_float(b, 2)
                    x_high(k, b, KT - 1, (b + 1) % 2)
                    a_float(b, 3)
                split_w(WQ, k)
                if kind == "prepare":
                    for i in range(4, KT):
                        a_float(b, i)
                split_w(WK, k)

            act.wait_ge(w_ld[0], 16)
            act.copy(w_hi[:, WQ], w_raw[:, 0]).then_inc(whi_done, 1)
            for i in range(KT):
                x_high(-1, -1, i, 0)
            act.wait_ge(const_ld, 48)
            act.activation(tg[:], gate_in[:], ACT.Tanh).then_inc(tg_done, 1)
            for i in range(KT):
                a_float(-1, i)
                if i == 1:
                    act.wait_ge(w_ld[1], 16)
                    act.copy(w_hi[:, WK], w_raw[:, 1]).then_inc(whi_done, 1)
            act.wait_ge(w_ld[0], 32)
            act.copy(w_hi[:, WV], w_raw[:, 0]).then_inc(whi_done, 1)
            q_high(-1, 0)
            q_high(-1, 1)
            act.wait_ge(w_ld[1], 32)
            act.copy(w_hi[:, WQ], w_raw[:, 1]).then_inc(whi_done, 1)
            for h in range(2):
                k_high(-1, h)
            act.wait_ge(w_ld[0], 48)
            act.copy(w_hi[:, WK], w_raw[:, 0]).then_inc(whi_done, 1)
            run_loops(act, body)

        @block.vector
        def _(dve):
            def row_max(k, u):
                dve.wait_ge(s_done, k * UNITS + (u + 1))
                dve.nop(nofuse=True)
                dve.wait_ge(mask_done, 2)
                dve.tensor_tensor_reduce(prob[:, u], so[u % 2][:], mask_add[:], -SCALE, BIG, ALU.add, ALU.min,
                                         nmax[:, u:u + 1]).then_inc(so_read, 1)

            def inverse_sums(k, i):
                dve.wait_ge(exp_done, k * UNITS + 2 * (i + 1))
                dve.reciprocal(rinv[:, 2 * i:2 * i + 2], rsum[:, 2 * i:2 * i + 2]).then_inc(rinv_done, 1)

            def v_low(k):
                dve.wait_ge(vh_done, k + 1)
                dve.tensor_tensor(v_st[:, :, 1:3], pj[0][:].rearrange("p (s h d) -> p s h d", s=TB, h=2),
                                  f32(v_st[:, :, 0:4:3]), ALU.subtract).then_inc(vl_done, 1)

            def q_low(k, h):
                dve.wait_ge(qh_done, k * 2 + (3 + h))
                src, dst = (hi_half, lo_half) if h else (lo_half, hi_half)
                dve.tensor_tensor(q_st[dst, h], pj[1][src], f32(q_st[src, h]), ALU.subtract).then_inc(ql_done, 1)

            def k_low(k, h):
                dve.wait_ge(kh_done, k * 2 + (3 + h))
                half = hi_half if h else lo_half
                dve.tensor_tensor(k_st[half, h, 1], pj[0][half], f32(k_st[half, h, 0]),
                                  ALU.subtract).then_inc(kl_done, 1)

            def p_low(k, u):
                dve.wait_ge(ph_done, k * UNITS + (u + 1))
                dve.tensor_tensor(pt_lo[:, u % 2], pt[u % 2][:], f32(pt_hi[:, u % 2]),
                                  ALU.subtract).then_inc(pl_done, 1)

            def o_add(k, h):
                dve.wait_ge(otmp_done, k * 2 + (h + 1))
                rows = hi_half if h else lo_half
                dve.tensor_tensor(o32[rows], pv[h][rows], o_tmp[rows], ALU.add).then_inc(oadd_done, 1)

            def o_low(k):
                dve.wait_ge(oh_done, k + 1)
                dve.tensor_tensor(o_lo[:], o32[:], f32(o_hi[:]), ALU.subtract).then_inc(ol_done, 1)

            def accumulate(k, n, parity):
                dve.wait_ge(op_done, k * KT + (n + 1))
                y = xy[:, bass.ds(parity, 1), n].rearrange("p a t -> p (a t)")
                dve.scalar_tensor_tensor(out=y, in0=po[n % 4][:], scalar=tg[:], in1=y,
                                         op0=ALU.mult, op1=ALU.add).then_inc(so_read, 1)

            def x_low(b, i, parity):
                dve.wait_ge(xh_done, b * KT + (KT + i + 1))
                dve.tensor_tensor(x_lo[:, i], xy[:, bass.ds(parity, 1), i].rearrange("p a t -> p (a t)"), f32(x_hi[:, i]),
                                  ALU.subtract).then_inc(xlv_done, 1)

            def a_low(b, i):
                dve.wait_ge(ah_done, b * KT + (KT + i + 1))
                dve.tensor_tensor(blocks(a_lo[:, i]), at(i), f32(blocks(a_hi[:, i])), ALU.subtract).then_inc(alv_done, 1)

            def build_mask(b):
                dve.wait_ge(mask_ld, b * 16 + 32)
                dve.tensor_scalar(mask_add[:], mask_u8[:], -1.0, BIG, ALU.add, ALU.mult).then_inc(mask_done, 1)
                dve.wait_ge(mask_done, b * 2 + 3)
                dve.tensor_scalar(mask_add[:], mask_add[:], BIG, None, ALU.mult).then_inc(mask_done, 1)
                dve.wait_ge(mask_done, b * 2 + 4)

            def row_stats(b, i):
                s, half = divmod(i, 2)
                if isinstance(b, int) and b == -1:
                    dve.wait_ge(ctx_first[s], 16)
                elif i == 0:
                    dve.wait_ge(ctx_ld, b * 64 + 64)
                dve.bn_stats(bn[:, s, half], cx[:, s, half * T:(half + 1) * T]).then_inc(bn_done, 1)

            def row_moments(b):
                dve.wait_ge(bn_done, b * 3 * TB + 5 * TB)
                dve.nop(nofuse=True)
                for s in range(TB):
                    dve.bn_aggr(mv[:, s], bn[:, s].rearrange("p a c -> p (a c)")).then_inc(bn_done, 1)
                dve.wait_ge(bn_done, b * 3 * TB + 6 * TB)
                dve.tensor_scalar(nmean[:], mv[:, :, 0], -1.0, None, ALU.mult).then_inc(stat_done, 1)
                dve.tensor_scalar(vpe[:], mv[:, :, 1], EPS, None, ALU.add).then_inc(stat_done, 1)

            def body(k, b, j, kind):
                last = kind == "last"
                parity = b % 2
                for u in range(UNITS):
                    row_max(k, u)
                    if u == 1:
                        v_low(k)
                    if u in (3, 5, 7):
                        inverse_sums(k, (u - 3) // 2)
                    if kind == "prepare":
                        row_stats(b, u)
                    if kind == "switch" and 2 <= u < 2 + BY_V:
                        a_low(b, u - 2)
                if not last:
                    q_low(k, 0)
                inverse_sums(k, 3)
                for u in range(UNITS):
                    p_low(k, u)
                    if u == 1 and not last:
                        q_low(k, 1)
                    if u == 1 and kind == "prepare":
                        row_moments(b)
                    if u == 5:
                        o_add(k, 0)
                    if kind == "switch" and u == 4:
                        build_mask(b)
                if not last and kind != "prepare":
                    k_low(k, 0)
                    k_low(k, 1)
                o_add(k, 1)
                o_low(k)
                for n in range(KT):
                    accumulate(k, n, parity)
                    if kind == "prepare" and n < 2:
                        k_low(k, n)
                    if kind == "prepare" and 2 <= n < 2 + BY_V:
                        x_low(b, n - 2, (b + 1) % 2)

            for i, s in enumerate((pl_done, pl_done, so_read, so_read, so_read, so_read)):
                dve.memset(nmax[:, i:i + 1], 0.0).then_inc(s, 1)
            for i in range(2 * TB):
                row_stats(-1, i)
            row_moments(-1)
            dve.wait_ge(rstd_done, 1)
            dve.nop(nofuse=True)
            for s in range(2):
                dve.tensor_scalar(cx[:, s], cx[:, s], nmean[:, s:s + 1], rstd[:, s:s + 1], ALU.add,
                                  ALU.mult).then_inc(z_done, 1)
            for i in range(BY_V):
                x_low(-1, i, 0)
            for i in range(KT):
                dve.wait_ge(at_done, i + 1)
                dve.tensor_copy(blocks(a_hi[:, i]), at(i)).then_inc(ah_done, 1)
                if i < BY_V:
                    a_low(-1, i)
            build_mask(-1)
            dve.wait_ge(tg_done, 1)
            q_low(-1, 0)
            q_low(-1, 1)
            for h in range(2):
                k_low(-1, h)
            run_loops(dve, body)

        @block.gpsimd
        def _(pool):
            def scale_rows(k, u):
                if u % 2 == 0:
                    pool.wait_ge(rinv_done, k * 4 + (u // 2 + 1))
                    pool.nop(nofuse=True)
                pool.tensor_scalar(prob[:, u], prob[:, u], rinv[:, u:u + 1], 1.0, ALU.mult,
                                   ALU.mult).then_inc(scale_done, 1)

            def split_w(kind, k, less=0):
                pool.wait_ge(whi_done, w_number(kind, k) + (1 - less))
                pool.tensor_tensor(w_lo[:, kind], w_raw[:, w_slot(kind)], f32(w_hi[:, kind]),
                                   ALU.subtract).then_inc(wlo_done, 1)

            def norm_rows(b, blocks=range(TB)):
                pool.wait_ge(stat_done, b * 2 + 4)
                pool.tensor_tensor(rstd[:], vpe[:], nhalf[:], ALU.pow).then_inc(rstd_done, 1)
                pool.wait_ge(rstd_done, b + 2)
                pool.nop(nofuse=True)
                for s in blocks:
                    pool.tensor_scalar(cx[:, s], cx[:, s], nmean[:, s:s + 1], rstd[:, s:s + 1], ALU.add,
                                       ALU.mult).then_inc(z_done, 1)

            def x_low(b, i, parity):
                pool.wait_ge(xh_done, b * KT + (KT + i + 1))
                pool.nop(nofuse=True)
                pool.tensor_tensor(x_lo[:, i], xy[:, bass.ds(parity, 1), i].rearrange("p a t -> p (a t)"),
                                   f32(x_hi[:, i]), ALU.subtract).then_inc(xlp_done, 1)

            def a_low(b, i):
                pool.wait_ge(ah_done, b * KT + (KT + i + 1))
                pool.tensor_tensor(blocks(a_lo[:, i]), at(i), f32(blocks(a_hi[:, i])),
                                   ALU.subtract).then_inc(alp_done, 1)

            def body(k, b, j, kind):
                for u in range(UNITS):
                    scale_rows(k, u)
                    if kind == "switch" and u in (3, 5, 7):
                        a_low(b, BY_V + (u - 3) // 2)
                if kind == "last":
                    return split_w(WO, k, less=1)
                if kind == "switch":
                    a_low(b, KT - 1)
                split_w(WV, k)
                if kind == "prepare":
                    norm_rows(b)
                split_w(WO, k)
                if kind == "prepare":
                    for i in range(BY_V, KT):
                        x_low(b, i, (b + 1) % 2)
                split_w(WQ, k)
                split_w(WK, k)

            pool.memset(ident[:], 0.0).then_inc(ident_done, 1)
            pool.memset(nhalf[:], -0.5).then_inc(nhalf_done, 1)
            pool.wait_ge(ident_done, 1)
            pool.affine_select(out=ident[:], in_=ident[:], compare_op=ALU.not_equal, fill=1.0, base=0,
                               pattern=[[-1, P]], channel_multiplier=1).then_inc(ident_done, 1)
            pool.wait_ge(nhalf_done, 1)

            def split_first(m, kind):
                pool.wait_ge(whi_done, m + 1)
                pool.tensor_tensor(w_lo[:, kind], w_raw[:, m % 2], f32(w_hi[:, kind]),
                                   ALU.subtract).then_inc(wlo_done, 1)

            split_first(0, WQ)
            norm_rows(-1, range(2, TB))
            for i in range(BY_V, KT):
                x_low(-1, i, 0)
            split_first(1, WK)
            for i in range(BY_V, KT):
                a_low(-1, i)
            for m, kind in ((2, WV), (3, WQ), (4, WK)):
                split_first(m, kind)
            run_loops(pool, body)


def kernel(**inputs):
    import concourse.bacc as bacc
    from concourse.bass_utils import run_bass_kernel_spmd

    def arr(name):
        return np.asarray(inputs[name])

    def lay(a):
        return np.ascontiguousarray(a)

    def projection(w):
        return lay(w.reshape(PAIRS, P, KT, P).transpose(0, 3, 2, 1)).reshape(PAIRS, P, D)

    arrays = {
        "xT": lay(arr("x").reshape(B, T, KT, P).transpose(0, 3, 2, 1)).reshape(B, P, KT * T),
        "ctx": lay(arr("ctx_2048")),
        "mask": lay(arr("mask_BxS2_bf1")).view(np.uint8),
        "wq": projection(arr("L0_xattn_Wq")),
        "wk": projection(arr("L0_xattn_Wk")),
        "wv": projection(arr("L0_xattn_Wv")),
        "wo": lay(arr("L0_xattn_Wo").T).reshape(PAIRS, P, D),
        "gamma": lay(arr("L0_xattn_ln_gamma").reshape(KT, P).T),
        "beta": lay(arr("L0_xattn_ln_beta").reshape(KT, P).T),
        "gate": lay(arr("L0_xattn_gate").reshape(1, 1)),
    }
    nc = bacc.Bacc("TRN2", target_bir_lowering=False, num_devices=1)
    t = {n: nc.dram_tensor(f"in_{n}", a.shape, mybir.dt.from_np(a.dtype), kind="ExternalInput").ap()
         for n, a in arrays.items()}
    y = nc.dram_tensor("out_y", (B, P, KT * T), F32, kind="ExternalOutput").ap()
    xattn_kernel(nc, t["xT"], t["ctx"], t["mask"], [t["wq"], t["wk"], t["wv"], t["wo"]],
                 t["gamma"], t["beta"], t["gate"], y)
    r = run_bass_kernel_spmd(nc, [{f"in_{n}": a for n, a in arrays.items()}], core_ids=[0])
    out = np.asarray(r.results[0]["out_y"]).reshape(B, P, KT, T).transpose(0, 3, 2, 1)
    return np.ascontiguousarray(out).reshape(B, T, D)
```
